# Optimizing a Trainium2 kernel written in Bass

```python
import numpy as np
import jax
import jax.numpy as jnp

def _softmax(x, axis=-1):
    return jax.nn.softmax(x, axis=axis)

def _gelu(x):
    return jax.nn.gelu(x, approximate=True)

def _silu(x):
    return jax.nn.silu(x)

def _sigmoid(x):
    return jax.nn.sigmoid(x)

def _layernorm(x, axis=-1, eps=1e-05):
    m = jnp.mean(x, axis=axis, keepdims=True)
    v = jnp.var(x, axis=axis, keepdims=True)
    return (x - m) / jnp.sqrt(v + eps)

def _scatter_add(tgt, idx, src, axis=0):
    return tgt.at[idx].add(src)

def _segment_sum(src, seg, n):
    return jax.ops.segment_sum(src, seg, n)
kernel_name = 'mk_seq_preln_d1_jaxref_r4_6b3f50'

def setup_inputs(seed: int=0):
    np.random.seed(seed)
    _w = jnp.asarray

    def _L0_attn_setup():
        import jax, jax.numpy as jnp
        import numpy as np
        DEPTH, DIM, DFF, VOCAB = (4, 128, 512, 1024)
        EPS = 1e-05

        def layernorm(x, w, b):
            mu = jnp.mean(x, axis=-1, keepdims=True)
            var = jnp.mean((x - mu) ** 2, axis=-1, keepdims=True)
            return (x - mu) * jax.lax.rsqrt(var + EPS) * w + b

        def sconv(x, phazor_c, last_conv_c):
            B, L, D = x.shape
            r = jnp.abs(phazor_c)
            p = jnp.tanh(r) * jnp.exp(1j * jnp.angle(phazor_c))
            prog = p[None, :] ** jnp.arange(L, dtype=jnp.float32)[:, None]
            filt_fft = jnp.fft.fft(prog, n=2 * L, axis=0)
            x_fft = jnp.fft.fft(x.astype(jnp.complex64), n=2 * L, axis=1)
            conv = jnp.fft.ifft(filt_fft[None] * x_fft, axis=1)[:, :L]
            conv = conv + last_conv_c[None, None, :] * prog[None] * p[None, None, :]
            return conv.real.astype(x.dtype)

        def _forward(x, Win, bin, ln1_w, ln1_b, phz_re, phz_im, lc_re, lc_im, sc_lin, ln2_w, ln2_b, W1, b1, W2, b2, lnl_w, lnl_b, Wout, bout):
            h = jnp.einsum('blv,dv->bld', x, Win) + bin

            def body(h, p):
                l1w, l1b, pr, pi, lr, li, scl, l2w, l2b, w1, b1_, w2, b2_ = p
                y = jax.nn.silu(layernorm(h, l1w, l1b))
                y = sconv(y, pr + 1j * pi, lr + 1j * li)
                h = h + y * scl
                y = layernorm(h, l2w, l2b)
                y = jax.nn.silu(jnp.einsum('bld,fd->blf', y, w1) + b1_)
                y = jnp.einsum('blf,df->bld', y, w2) + b2_
                return (h + y, None)
            xs = (ln1_w, ln1_b, phz_re, phz_im, lc_re, lc_im, sc_lin, ln2_w, ln2_b, W1, b1, W2, b2)
            h, _ = jax.lax.scan(body, h, xs)
            h = layernorm(h, lnl_w, lnl_b)
            return jnp.einsum('bld,vd->blv', h, Wout) + bout
        key = jax.random.key(seed)
        ks = jax.random.split(key, 20)
        f32 = jnp.float32
        inp = {}
        inp['x'] = jax.random.normal(ks[0], (2, 1024, VOCAB), dtype=f32)
        inp['Win'] = jax.random.normal(ks[1], (DIM, VOCAB), dtype=f32) * VOCAB ** (-0.5)
        inp['bin'] = jnp.zeros((DIM,), f32)
        inp['ln1_w'] = jnp.ones((DEPTH, DIM), f32)
        inp['ln1_b'] = jnp.zeros((DEPTH, DIM), f32)
        ang = 2 * np.pi * jnp.arange(DIM, dtype=f32) / DIM
        mag = jnp.abs(jax.random.normal(ks[2], (DEPTH, DIM), dtype=f32))
        inp['phz_re'] = mag * jnp.cos(ang)[None]
        inp['phz_im'] = mag * jnp.sin(ang)[None]
        inp['lc_re'] = jax.random.normal(ks[3], (DEPTH, DIM), dtype=f32)
        inp['lc_im'] = jax.random.normal(ks[4], (DEPTH, DIM), dtype=f32)
        inp['sc_lin'] = jnp.ones((DEPTH, DIM), f32)
        inp['ln2_w'] = jnp.ones((DEPTH, DIM), f32)
        inp['ln2_b'] = jnp.zeros((DEPTH, DIM), f32)
        inp['W1'] = jax.random.normal(ks[5], (DEPTH, DFF, DIM), dtype=f32) * DIM ** (-0.5)
        inp['b1'] = jnp.zeros((DEPTH, DFF), f32)
        inp['W2'] = jax.random.normal(ks[6], (DEPTH, DIM, DFF), dtype=f32) * DFF ** (-0.5)
        inp['b2'] = jnp.zeros((DEPTH, DIM), f32)
        inp['lnl_w'] = jnp.ones((DIM,), f32)
        inp['lnl_b'] = jnp.zeros((DIM,), f32)
        inp['Wout'] = jax.random.normal(ks[7], (VOCAB, DIM), dtype=f32) * DIM ** (-0.5)
        inp['bout'] = jnp.zeros((VOCAB,), f32)
        return inp
    _L0_attn_in = _L0_attn_setup()

    def _L0_ffn_setup():
        import jax, jax.numpy as jnp
        import numpy as np
        B, S = (4, 512)
        IN, OUT = (1024, 1024)
        SPARSITY = 0.05
        ALPHA = 1.0

        def _dequant(base_packed, scales):
            low = base_packed & 15
            high = base_packed >> 4 & 15
            offs = jnp.stack([low, high], axis=-1).reshape(base_packed.shape[0], -1)
            return (offs.astype(jnp.float32) - 8.0) * scales
        key = jax.random.key(seed)
        k1, k2, k3, k4, k5 = jax.random.split(key, 5)
        x = jax.random.normal(k1, (B, S, IN), dtype=jnp.float32)
        base_packed = jax.random.randint(k2, (OUT, IN // 2), 0, 64, dtype=jnp.int32)
        scales = jax.random.uniform(k3, (OUT, 1), dtype=jnp.float32, minval=0.001, maxval=0.02)
        mask = jax.random.bernoulli(k4, SPARSITY, (OUT, IN))
        w_ortho = jax.random.normal(k5, (OUT, IN), dtype=jnp.float32) * 0.01 * mask
        return {'x': x, 'base_packed': base_packed, 'scales': scales, 'w_ortho': w_ortho}
    _L0_ffn_in = _L0_ffn_setup()
    _d = {'L0_attn_x': _L0_attn_in['x'], 'L0_attn_Win': _L0_attn_in['Win'], 'L0_attn_bin': _L0_attn_in['bin'], 'L0_attn_ln1_w': _L0_attn_in['ln1_w'], 'L0_attn_ln1_b': _L0_attn_in['ln1_b'], 'L0_attn_phz_re': _L0_attn_in['phz_re'], 'L0_attn_phz_im': _L0_attn_in['phz_im'], 'L0_attn_lc_re': _L0_attn_in['lc_re'], 'L0_attn_lc_im': _L0_attn_in['lc_im'], 'L0_attn_sc_lin': _L0_attn_in['sc_lin'], 'L0_attn_ln2_w': _L0_attn_in['ln2_w'], 'L0_attn_ln2_b': _L0_attn_in['ln2_b'], 'L0_attn_W1': _L0_attn_in['W1'], 'L0_attn_b1': _L0_attn_in['b1'], 'L0_attn_W2': _L0_attn_in['W2'], 'L0_attn_b2': _L0_attn_in['b2'], 'L0_attn_lnl_w': _L0_attn_in['lnl_w'], 'L0_attn_lnl_b': _L0_attn_in['lnl_b'], 'L0_attn_Wout': _L0_attn_in['Wout'], 'L0_attn_bout': _L0_attn_in['bout'], 'L0_ffn_base_packed': _L0_ffn_in['base_packed'], 'L0_ffn_scales': _L0_ffn_in['scales'], 'L0_ffn_w_ortho': _L0_ffn_in['w_ortho']}
    _x0 = _d['L0_attn_x']
    _d['L0_attn_x'] = jax.random.normal(jax.random.fold_in(jax.random.key(seed), 1), (2, 2048, 1024), dtype=_x0.dtype)
    del _x0
    return _d

def reference(L0_attn_x, L0_attn_Win, L0_attn_bin, L0_attn_ln1_w, L0_attn_ln1_b, L0_attn_phz_re, L0_attn_phz_im, L0_attn_lc_re, L0_attn_lc_im, L0_attn_sc_lin, L0_attn_ln2_w, L0_attn_ln2_b, L0_attn_W1, L0_attn_b1, L0_attn_W2, L0_attn_b2, L0_attn_lnl_w, L0_attn_lnl_b, L0_attn_Wout, L0_attn_bout, L0_ffn_base_packed, L0_ffn_scales, L0_ffn_w_ortho):

    def _L0_attn_ref(x, Win, bin, ln1_w, ln1_b, phz_re, phz_im, lc_re, lc_im, sc_lin, ln2_w, ln2_b, W1, b1, W2, b2, lnl_w, lnl_b, Wout, bout):
        import jax, jax.numpy as jnp
        import numpy as np
        DEPTH, DIM, DFF, VOCAB = (4, 128, 512, 1024)
        EPS = 1e-05

        def layernorm(x, w, b):
            mu = jnp.mean(x, axis=-1, keepdims=True)
            var = jnp.mean((x - mu) ** 2, axis=-1, keepdims=True)
            return (x - mu) * jax.lax.rsqrt(var + EPS) * w + b

        def sconv(x, phazor_c, last_conv_c):
            B, L, D = x.shape
            r = jnp.abs(phazor_c)
            p = jnp.tanh(r) * jnp.exp(1j * jnp.angle(phazor_c))
            prog = p[None, :] ** jnp.arange(L, dtype=jnp.float32)[:, None]
            filt_fft = jnp.fft.fft(prog, n=2 * L, axis=0)
            x_fft = jnp.fft.fft(x.astype(jnp.complex64), n=2 * L, axis=1)
            conv = jnp.fft.ifft(filt_fft[None] * x_fft, axis=1)[:, :L]
            conv = conv + last_conv_c[None, None, :] * prog[None] * p[None, None, :]
            return conv.real.astype(x.dtype)

        def _forward(x, Win, bin, ln1_w, ln1_b, phz_re, phz_im, lc_re, lc_im, sc_lin, ln2_w, ln2_b, W1, b1, W2, b2, lnl_w, lnl_b, Wout, bout):
            h = jnp.einsum('blv,dv->bld', x, Win) + bin

            def body(h, p):
                l1w, l1b, pr, pi, lr, li, scl, l2w, l2b, w1, b1_, w2, b2_ = p
                y = jax.nn.silu(layernorm(h, l1w, l1b))
                y = sconv(y, pr + 1j * pi, lr + 1j * li)
                h = h + y * scl
                y = layernorm(h, l2w, l2b)
                y = jax.nn.silu(jnp.einsum('bld,fd->blf', y, w1) + b1_)
                y = jnp.einsum('blf,df->bld', y, w2) + b2_
                return (h + y, None)
            xs = (ln1_w, ln1_b, phz_re, phz_im, lc_re, lc_im, sc_lin, ln2_w, ln2_b, W1, b1, W2, b2)
            h, _ = jax.lax.scan(body, h, xs)
            h = layernorm(h, lnl_w, lnl_b)
            return jnp.einsum('bld,vd->blv', h, Wout) + bout
        return _forward(x, Win, bin, ln1_w, ln1_b, phz_re, phz_im, lc_re, lc_im, sc_lin, ln2_w, ln2_b, W1, b1, W2, b2, lnl_w, lnl_b, Wout, bout)

    def _L0_ffn_ref(x, base_packed, scales, w_ortho):
        import jax, jax.numpy as jnp
        import numpy as np
        B, S = (4, 512)
        IN, OUT = (1024, 1024)
        SPARSITY = 0.05
        ALPHA = 1.0

        def _dequant(base_packed, scales):
            low = base_packed & 15
            high = base_packed >> 4 & 15
            offs = jnp.stack([low, high], axis=-1).reshape(base_packed.shape[0], -1)
            return (offs.astype(jnp.float32) - 8.0) * scales
        w = _dequant(base_packed, scales) + ALPHA * w_ortho
        return jnp.einsum('bsi,oi->bso', x, w)
    x = L0_attn_x
    x = x + _L0_attn_ref(_layernorm(x, axis=-1), L0_attn_Win, L0_attn_bin, L0_attn_ln1_w, L0_attn_ln1_b, L0_attn_phz_re, L0_attn_phz_im, L0_attn_lc_re, L0_attn_lc_im, L0_attn_sc_lin, L0_attn_ln2_w, L0_attn_ln2_b, L0_attn_W1, L0_attn_b1, L0_attn_W2, L0_attn_b2, L0_attn_lnl_w, L0_attn_lnl_b, L0_attn_Wout, L0_attn_bout)
    x = x + _L0_ffn_ref(_layernorm(x, axis=-1), L0_ffn_base_packed, L0_ffn_scales, L0_ffn_w_ortho)
    return x

_drawn_inputs = setup_inputs


def setup_inputs(seed=0):
    import zlib

    import numpy as np

    out = dict(_drawn_inputs(seed))
    spreads = {'L0_attn_bin': (0.0, 0.1),
     'L0_attn_ln1_w': (1.0, 0.2),
     'L0_attn_ln1_b': (0.0, 0.1),
     'L0_attn_sc_lin': (1.0, 0.2),
     'L0_attn_ln2_w': (1.0, 0.2),
     'L0_attn_ln2_b': (0.0, 0.337),
     'L0_attn_b1': (0.0, 0.327),
     'L0_attn_b2': (0.0, 0.1),
     'L0_attn_lnl_w': (1.0, 0.2),
     'L0_attn_lnl_b': (0.0, 0.1),
     'L0_attn_bout': (0.0, 0.1)}
    factors = {'L0_attn_lc_re': 3.841, 'L0_attn_lc_im': 4.798}
    for name, (base, spread) in spreads.items():
        noise = np.random.default_rng([zlib.crc32(name.encode()), seed]).standard_normal(out[name].shape)
        drawn = base * np.exp(spread * noise) if base else spread * noise
        out[name] = jnp.asarray(drawn.astype(out[name].dtype))
    for name, factor in factors.items():
        out[name] = (out[name] * factor).astype(out[name].dtype)
    return out
```

```python
import concourse.bass as bass
from concourse import mybir
from contextlib import ExitStack

_INS = ['L0_attn_x', 'L0_attn_Win', 'L0_attn_bin', 'L0_attn_ln1_w', 'L0_attn_ln1_b', 'L0_attn_phz_re',
        'L0_attn_phz_im', 'L0_attn_lc_re', 'L0_attn_lc_im', 'L0_attn_sc_lin', 'L0_attn_ln2_w', 'L0_attn_ln2_b',
        'L0_attn_W1', 'L0_attn_b1', 'L0_attn_W2', 'L0_attn_b2', 'L0_attn_lnl_w', 'L0_attn_lnl_b',
        'L0_attn_Wout', 'L0_attn_bout', 'L0_ffn_base_packed', 'L0_ffn_scales', 'L0_ffn_w_ortho']
_OUTS = [((2, 2048, 1024), 'float32')]


def sequence_block(nc, x, Win, bin_, ln1_w, ln1_b, phz_re, phz_im, lc_re, lc_im, sc_lin, ln2_w, ln2_b,
                   W1, b1, W2, b2, lnl_w, lnl_b, Wout, bout, packed, scales, ortho, out):
    fp32, f32r, i32 = mybir.dt.float32, mybir.dt.float32r, mybir.dt.int32
    ALU, ACT = mybir.AluOpType, mybir.ActivationFunctionType
    EPS = 1e-5

    P = nc.NUM_PARTITIONS
    BATCH, LEN, V = x.shape
    LAYERS, FF, D = W1.shape
    CHUNK = 512
    R = CHUNK // P
    CHUNKS = LEN // CHUNK
    STAGES_PER_CHUNK = LAYERS * BATCH
    TILES_PER_CHUNK = R * BATCH
    STAGES = CHUNKS * STAGES_PER_CHUNK
    TILES = CHUNKS * TILES_PER_CHUNK
    K = V // P
    KH = K // 2
    HALF = V // 2
    FT = FF // P
    OT = ortho.shape[0] // P
    AHEAD = TILES_PER_CHUNK
    MID, BACK = STAGES_PER_CHUNK + 1, STAGES_PER_CHUNK + 2
    assert STAGES_PER_CHUNK == TILES_PER_CHUNK == OT and BATCH == 2 and D == P

    SLOTS = range(-AHEAD, TILES + BACK + 1)

    def mixer_of(n):
        return n if 0 <= n < STAGES else None

    def mlp_of(n):
        return n - 1 if 0 <= n - 1 < STAGES else None

    def final_of(n):
        chunk, s = n // STAGES_PER_CHUNK - 1, n % STAGES_PER_CHUNK
        return BATCH * chunk + s if s < BATCH and 0 <= chunk < CHUNKS else None

    def front_of(n):
        return n + AHEAD if n + AHEAD < TILES else None

    def middle_of(n):
        return n - MID if 0 <= n - MID < TILES else None

    def back_of(n):
        return n - BACK if 0 <= n - BACK < TILES else None

    def weight_of(n):
        return n - 1 if 0 <= n - 1 < OT else None

    def layer(stage):
        return stage % STAGES_PER_CHUNK // BATCH

    def stream(stage):
        return stage % BATCH

    def rows(dram, tile):
        chunk, g = divmod(tile, TILES_PER_CHUNK)
        first = chunk * CHUNK + g % R * P
        return dram[g // R, first:first + P, :]

    PREP = {-7: [("Win", 0), ("Win", 1)], -6: [("Wout", 0), ("Wout", 1)], -3: [("W1", l) for l in range(LAYERS)],
            -1: [("W2", l) for l in range(LAYERS)]}

    A_TOK, C_TOK, FEAT, FF0, FF1, ACC, PAIR0, PAIR1 = range(8)
    TURN, turns = {}, [0] * 8

    def take(bank, key):
        TURN[key] = (bank, turns[bank])
        turns[bank] += 1

    take(PAIR1, ("params",))
    for n in SLOTS:
        m, c, g = mixer_of(n), mlp_of(n), final_of(n)
        f, mid, bk, w = front_of(n), middle_of(n), back_of(n), weight_of(n)
        if c is not None:
            take(C_TOK, ("mlp tokens", c))
        if m is not None:
            take(A_TOK, ("mixer tokens", m))
        if g is not None:
            take(FF0, ("final tokens", g))
        if bk is not None:
            take(PAIR0, ("back", bk, 0))
        if c is not None:
            take(FF1, ("mlp features", c))
        if mid is not None:
            take(PAIR1, ("Wout", mid, 0))
            take(ACC, ("Wout", mid, 1))
        if m is not None:
            take(FEAT, ("mixer features", m))
        if bk is not None:
            take(PAIR1, ("back", bk, 1))
        if c is not None:
            for j in range(FT):
                take((FF0, FF1)[j % 2], ("W1", c, j))
            take(ACC, ("W2", c))
        if f is not None:
            take(A_TOK, ("front", f, 0))
            take(C_TOK, ("front", f, 1))
        if g is not None:
            take(FEAT, ("final features", g))
        if mid is not None:
            take(FF0, ("middle", mid, 0))
            take(FF1, ("middle", mid, 1))
        if w is not None:
            take(PAIR0, ("weight", w, 0))
            take(PAIR1, ("weight", w, 1))
        for i, what in enumerate(PREP.get(n, [])):
            take((PAIR0, PAIR1)[i % 2], ("prep",) + what)
        if f is not None and f % 2 == 1:
            take(ACC, ("Win", f // 2))

    vectors = [("phz_re", phz_re), ("phz_im", phz_im), ("lc_re", lc_re), ("lc_im", lc_im),
               ("bin", bin_.rearrange("(a d) -> a d", a=1)), ("ln1_w", ln1_w), ("ln1_b", ln1_b),
               ("scl", sc_lin), ("ln2_w", ln2_w), ("ln2_b", ln2_b),
               ("b1", b1.rearrange("l (j p) -> (l j) p", p=P)), ("b2", b2),
               ("lnl_w", lnl_w.rearrange("(a d) -> a d", a=1)),
               ("lnl_b", lnl_b.rearrange("(a d) -> a d", a=1)),
               ("scales", scales.rearrange("(t p) a -> (t a) p", p=P))]
    PAR, NPAR = {}, 0
    for name, v in vectors:
        PAR[name] = NPAR
        NPAR += v.shape[0]

    with ExitStack() as ctx:
        def sb(name, shape, dt=fp32):
            return ctx.enter_context(nc.sbuf_tensor(name, shape, dt))

        def sem(name):
            return ctx.enter_context(nc.semaphore(name))

        ident = sb("ident", [P, P])
        minus_half = sb("minus_half", [P, R])
        par = sb("par", [P, NPAR])
        bout_rows = sb("bout_rows", [P, V])
        WinT = sb("WinT", [P, K, P])
        W1_hi = sb("W1_hi", [P, LAYERS, FF], f32r)
        W1_lo = sb("W1_lo", [P, LAYERS, FF], f32r)
        W2T = sb("W2T", [P, LAYERS, FT, P])
        Wout_hi = sb("Wout_hi", [P, V], f32r)
        Wout_lo = sb("Wout_lo", [P, V], f32r)
        w_hi = sb("w_hi", [P, K, V], f32r)
        w_lo = sb("w_lo", [P, K, V], f32r)
        LEVELS = CHUNK.bit_length() - 1
        SHARED_LEVELS = 6
        turn = sb("turn", [P, LAYERS, 2, CHUNK])
        power = sb("power", [P, LEVELS + 1, 2, LAYERS])
        decay = sb("decay", [P, LAYERS])
        state = sb("state", [P, LAYERS, BATCH, 2])
        small = sb("small", [P, 16, LAYERS])
        xin = sb("xin", [P, 2, V])
        xT = sb("xT", [P, K, 2 * P])
        xr = sb("xr", [P, 4, V])
        x_hi = sb("x_hi", [P, 2, K, P], f32r)
        x_lo = sb("x_lo", [P, 2, K, P], f32r)
        h_in = sb("h_in", [P, BATCH, CHUNK])
        h = sb("h", [P, BATCH, CHUNK])
        fin_hi = sb("fin_hi", [P, BATCH, CHUNK], f32r)
        fin_lo = sb("fin_lo", [P, BATCH, CHUNK], f32r)
        normed = sb("normed", [P, 2, R, P])
        y = sb("y", [P, CHUNK])
        z = sb("z", [P, 2, CHUNK])
        yn = sb("yn", [P, CHUNK])
        yn_hi = sb("yn_hi", [P, CHUNK], f32r)
        yn_lo = sb("yn_lo", [P, CHUNK], f32r)
        ff = sb("ff", [P, 2, CHUNK])
        bn = sb("bn", [P, 3, R, 6])
        mv = sb("mv", [P, 3, R, 2])
        var = sb("var", [P, 3, R])
        rstd = sb("rstd", [P, 3, R])
        shift = sb("shift", [P, 3, R])
        bn_w = sb("bn_w", [P, 2, 2, 6])
        mv_w = sb("mv_w", [P, 2, 2, 2])
        var_w = sb("var_w", [P, 2, 2])
        rstd_w = sb("rstd_w", [P, 2, 2])
        shift_w = sb("shift_w", [P, 2, 2])
        par_rows = h[0:NPAR, 0, 0:P]
        xr_flat = xr[:, :, :].rearrange("p a v -> p (a v)")
        W1_nat = xr_flat[:, 0:2 * V].rearrange("p (l j d) -> p l j d", l=LAYERS, j=FT)
        W2_nat = xr_flat[:, 2 * V:4 * V].rearrange("p (l f) -> p l f", l=LAYERS)
        Win_nat = z[:, :, :].rearrange("p a t -> p (a t)")
        Wout_nat = normed[:, :, :, :].rearrange("p a r d -> p (a r) d")
        w_nat = [xr[:, 0, :], xr[:, 1, :]]
        nibbles_in = [xr[:, 2, i * HALF:(i + 1) * HALF].bitcast(i32) for i in range(2)]
        offsets = xr[:, 3, :].bitcast(i32).rearrange("p (i two) -> p i two", two=2)
        w_deq = xr[:, 3, :]
        xhat = z[:, :, :].rearrange("p a t -> p (a t)")
        minus_8_scales = sb("minus_8_scales", [P, OT])

        bank = [ctx.enter_context(nc.psum_tensor(f"bank{i}", [P, CHUNK], fp32)) for i in range(8)]
        filled = [sem(f"bank{i}_filled") for i in range(8)]
        drained = [sem(f"bank{i}_drained") for i in range(8)]

        params_loaded, bout_loaded = sem("params_loaded"), sem("bout_loaded")
        nat_loaded = {k: sem(f"{k}_loaded") for k in ("Win", "W1", "W2", "Wout")}
        x_loaded = [sem(f"x_loaded{i}") for i in range(2)]
        x_first_loaded = [sem(f"x_first_loaded{i}") for i in range(4)]
        xr_loaded = [sem(f"xr_loaded{i}") for i in range(4)]
        w_loaded = [sem(f"w_loaded{i}") for i in range(2)]
        stored = [sem(f"stored{i}") for i in range(4)]
        ident_zeroed, ident_ready = sem("ident_zeroed"), sem("ident_ready")
        par_ready, modulus_squared, modulus_root = sem("par_ready"), sem("modulus_squared"), sem("modulus_root")
        modulus_ready, decay_ready = sem("modulus_ready"), sem("decay_ready")
        var_ready = [sem(f"var_ready{i}") for i in range(3)]
        rstd_ready = [sem(f"rstd_ready{i}") for i in range(3)]
        shift_ready = [sem(f"shift_ready{i}") for i in range(3)]
        y_rotated, mixed = sem("y_rotated"), sem("mixed")
        yn_hi_ready, yn_lo_ready, fin_hi_ready, fin_lo_ready = (
            sem(q) for q in ("yn_hi_ready", "yn_lo_ready", "fin_hi_ready", "fin_lo_ready"))
        ff_used = sem("ff_used")
        powers_ready, table_step, tables_ready = sem("powers_ready"), sem("table_step"), sem("tables_ready")
        prep_hi_ready, offsets_ready, deq_ready = sem("prep_hi_ready"), sem("offsets_ready"), sem("deq_ready")
        var_w_ready = [sem(f"var_w_ready{i}") for i in range(2)]
        rstd_w_ready = [sem(f"rstd_w_ready{i}") for i in range(2)]
        shift_w_ready = [sem(f"shift_w_ready{i}") for i in range(2)]
        xhat_ready = [sem(f"xhat_ready{i}") for i in range(2)]
        xr_biased = sem("xr_biased")
        x_hi_ready = sem("x_hi_ready")
        w_ready, w_hi_ready = sem("w_ready"), sem("w_hi_ready")
        vec_step = sem("vec_step")

        def front_buffer(t):
            return xr[:, t, :] if t < 4 else xin[:, t % 2, :]

        def col(name, i=0):
            return par[:, PAR[name] + i:PAR[name] + i + 1]

        TOKENS = ["mixer tokens", "mlp tokens", "final tokens"]
        FEATURES = ["mixer features", "mlp features", "final features"]

        def norms(n):
            return [(i, s) for i, s in ((1, mlp_of(n)), (0, mixer_of(n)), (2, final_of(n))) if s is not None]

        def front_stats(f):
            return [] if f is None else [q for q in ((0, 1) if f == 0 else (f + 1,)) if q < TILES]

        SPLIT = [q for n in sorted(PREP) for q in PREP[n] if q[0] in ("W1", "Wout")]

        block = ctx.enter_context(nc.Block())

        @block.sync
        def _(sp):
            for t in range(6):
                if t == 2:
                    sp.dma_start(Win_nat, Win).then_inc(nat_loaded["Win"], 16)
                sp.dma_start(front_buffer(t), rows(x, t)).then_inc(x_first_loaded[t] if t < 4 else x_loaded[t % 2], 16)
            sp.dma_start(Wout_nat, Wout.rearrange("(j p) d -> p j d", p=P)).then_inc(nat_loaded["Wout"], 16)

            def load_weight(t):
                if t < OT:
                    sp.dma_start(w_nat[t % 2], ortho[t * P:(t + 1) * P, :]).then_inc(w_loaded[t % 2], 16)
                    sp.dma_start(nibbles_in[t % 2], packed[t * P:(t + 1) * P, :]).then_inc(w_loaded[t % 2], 16)

            def load_middle(t):
                if 0 <= t < TILES:
                    if t < 4:
                        b, k = TURN["weight", OT - 1 if t else OT - 2, 1]
                        sp.wait_ge(filled[b], k + 1)
                    else:
                        sp.wait_ge(stored[t % 4], 16 * (t // 4))
                    sp.dma_start(xr[:, t % 4, :], rows(x, t)).then_inc(xr_loaded[t % 4], 16)

            for n in SLOTS:
                if n == 0:
                    for i in range(LAYERS - 2, LAYERS):
                        b, k = TURN["prep", "W2", i]
                        sp.wait_ge(filled[b], k + 1)
                    load_weight(0)
                    load_weight(1)
                f, bk, w = front_of(n), back_of(n), weight_of(n)
                if f == 1 or f == 3:
                    b, k = TURN["front", f, 1]
                    sp.wait_ge(filled[b], k + 1)
                    if f == 1:
                        sp.dma_start(W1_nat, W1.rearrange("l (j p) d -> p l j d", p=P)).then_inc(nat_loaded["W1"], 16)
                    else:
                        sp.dma_start(W2_nat, W2.rearrange("l d f -> d l f")).then_inc(nat_loaded["W2"], 16)
                if f is not None and f >= 4 and f + 2 < TILES:
                    b, k = TURN["front", f, 1]
                    sp.wait_ge(filled[b], k + 1)
                    sp.dma_start(xin[:, f % 2, :], rows(x, f + 2)).then_inc(x_loaded[f % 2], 16)
                if w is not None:
                    b, k = TURN["weight", w, 1]
                    sp.wait_ge(filled[b], k + 1)
                    load_weight(w + 2)
                if bk is not None:
                    b, k = TURN["back", bk, 1]
                    sp.wait_ge(drained[b], k + 1)
                    sp.dma_start(rows(out, bk), xr[:, bk % 4, :]).then_inc(stored[bk % 4], 16)
                if n == LAYERS - 1:
                    sp.wait_ge(tables_ready, 1)
                    sp.dma_start(bout_rows[:, :], bout.rearrange("(a v) -> a v", a=1).to_broadcast([P, V])).then_inc(bout_loaded, 16)
                load_middle(n - MID + 2)
            for i in range(4):
                sp.wait_ge(stored[i], 16 * (TILES // 4))

        @block.gpsimd
        def _(pool):
            nc.gpsimd.memset(ident[:, :], 0.0).then_inc(ident_zeroed, 1)
            nc.gpsimd.memset(minus_half[:, :], -0.5).then_inc(ident_zeroed, 1)
            pool.wait_ge(ident_zeroed, 2)
            nc.gpsimd.affine_select(out=ident[:, :], in_=ident[:, :], compare_op=ALU.not_equal, fill=1.0, base=0,
                                    pattern=[[-1, P]], channel_multiplier=1).then_inc(ident_ready, 1)

            def root_w(i, tile):
                pool.wait_ge(var_w_ready[i], tile + 1)
                if tile >= 2:
                    pool.wait_ge(xhat_ready[i], tile - 1)
                nc.gpsimd.tensor_tensor(rstd_w[:, i, tile % 2:tile % 2 + 1], var_w[:, i, tile % 2:tile % 2 + 1],
                                        minus_half[:, 0:1],
                                        ALU.pow).then_inc(rstd_w_ready[i], 1)

            def bias(mid):
                if mid is not None:
                    if mid == 0:
                        pool.wait_ge(bout_loaded, 16)
                    pool.wait_ge(xr_loaded[mid % 4], 16 * (mid // 4 + 1))
                    nc.gpsimd.tensor_tensor(xr[:, mid % 4, :], xr[:, mid % 4, :], bout_rows[:, :],
                                            ALU.add).then_inc(xr_biased, 1)

            for n in SLOTS:
                f, mid, w = front_of(n), middle_of(n), weight_of(n)
                for i, q in norms(n):
                    pool.wait_ge(var_ready[i], q + 1)
                    nc.gpsimd.tensor_tensor(rstd[:, i, :], var[:, i, :], minus_half[:, :],
                                            ALU.pow).then_inc(rstd_ready[i], 1)
                for q in front_stats(f):
                    root_w(0, q)
                if f == 1:
                    pool.wait_ge(modulus_squared, 1)
                    nc.gpsimd.tensor_tensor(small[:, 1, :], small[:, 0, :], minus_half[:, 0:LAYERS],
                                            ALU.pow).then_inc(modulus_root, 1)
                if mid is not None:
                    root_w(1, mid)
                bias(middle_of(n + 1))
                if w is not None:
                    pool.wait_ge(deq_ready, w + 1)
                    pool.wait_ge(w_loaded[w % 2], 32 * (w // 2 + 1))
                    nc.gpsimd.tensor_tensor(w_nat[w % 2], w_deq, w_nat[w % 2], ALU.add).then_inc(w_ready, 1)

        @block.scalar
        def _(act):
            for name, v in vectors:
                act.dma_start(par_rows[PAR[name]:PAR[name] + v.shape[0], :], v).then_inc(params_loaded, 16)

            def norm_w(i, tile, dst, src):
                act.wait_ge(shift_w_ready[i], tile + 1)
                nc.scalar.activation(dst, src, ACT.Identity, bias=shift_w[:, i, tile % 2:tile % 2 + 1],
                                     scale=rstd_w[:, i, tile % 2:tile % 2 + 1]).then_inc(xhat_ready[i], 1)

            def normalise(i, q, n):
                b, k = TURN[TOKENS[i], q]
                act.wait_ge(shift_ready[i], q + 1)
                lane = min(i, 1)
                if i == 2 and mlp_of(n) is not None:
                    bf, kf = TURN["mlp features", mlp_of(n)]
                    act.wait_ge(filled[bf], kf + 1)
                elif i == 1 and final_of(n - 1) is not None:
                    bf, kf = TURN["final features", final_of(n - 1)]
                    act.wait_ge(filled[bf], kf + 1)
                elif q > 0:
                    bf, kf = TURN[FEATURES[i], q - 1]
                    act.wait_ge(filled[bf], kf + 1)
                for r in range(R):
                    last = nc.scalar.activation(normed[:, lane, r, :], bank[b][:, r * P:(r + 1) * P], ACT.Identity,
                                                bias=shift[:, i, r:r + 1], scale=rstd[:, i, r:r + 1])
                last.then_inc(drained[b], 1)

            def front_out(f, u):
                b, k = TURN["front", f, u]
                act.wait_ge(filled[b], k + 1)
                if f % 2 == 0 and f >= 2:
                    bw, kw = TURN["Win", f // 2 - 1]
                    act.wait_ge(filled[bw], kw + 1)
                nc.scalar.activation(xT[:, u * KH:(u + 1) * KH, f % 2 * P:(f % 2 + 1) * P],
                                     bank[b][:, :].rearrange("p (k t) -> p k t", k=KH),
                                     ACT.Copy).then_inc(drained[b], 1)

            prep_to = {"Win": lambda i: WinT[:, i * KH:(i + 1) * KH, :].rearrange("p k d -> p (k d)"),
                       "W1": lambda i: W1_hi[:, i, :], "W2": lambda i: W2T[:, i, :, :].rearrange("p j d -> p (j d)"),
                       "Wout": lambda i: Wout_hi[:, i * HALF:(i + 1) * HALF]}

            for n in SLOTS:
                m, c, g = mixer_of(n), mlp_of(n), final_of(n)
                f, mid, w = front_of(n), middle_of(n), weight_of(n)
                if c is not None:
                    normalise(1, c, n)
                if m is not None:
                    normalise(0, m, n)
                if c is not None:
                    b, k = TURN["mlp features", c]
                    act.wait_ge(filled[b], k + 1)
                    if c > 0:
                        bw, kw = TURN["W1", c - 1, FT - 1]
                        act.wait_ge(filled[bw], kw + 1)
                    nc.scalar.activation(yn_hi[:, :], bank[b][:, :], ACT.Identity, bias=col("ln2_b", layer(c)),
                                         scale=col("ln2_w", layer(c))).then_inc(yn_hi_ready, 1)
                    if c > 0:
                        act.wait_ge(yn_lo_ready, c)
                        if final_of(n - 1) is not None:
                            act.wait_ge(fin_lo_ready, final_of(n - 1) + 1)
                    nc.scalar.activation(yn[:, :], bank[b][:, :], ACT.Identity, bias=col("ln2_b", layer(c)),
                                         scale=col("ln2_w", layer(c))).then_inc(drained[b], 1)
                if m is not None:
                    b, k = TURN["mixer features", m]
                    act.wait_ge(filled[b], k + 1)
                    if m > 0:
                        act.wait_ge(y_rotated, 2 * m)
                    nc.scalar.activation(y[:, :], bank[b][:, :], ACT.Silu, bias=col("ln1_b", layer(m)),
                                         scale=col("ln1_w", layer(m))).then_inc(drained[b], 1)
                if g is not None:
                    normalise(2, g, n)
                if f is not None:
                    norm_w(0, f, front_buffer(f), front_buffer(f))
                if c is None and f is not None:
                    front_out(f, 0)
                    front_out(f, 1)
                if c is not None:
                    for j in range(FT):
                        b, k = TURN["W1", c, j]
                        act.wait_ge(filled[b], k + 1)
                        if j >= 2:
                            act.wait_ge(ff_used, (FT - 1) * c + j - 1)
                        elif c > 0:
                            bw, kw = TURN["W2", c - 1]
                            act.wait_ge(filled[bw], kw + 1)
                        nc.scalar.activation(ff[:, j % 2, :], bank[b][:, :], ACT.Silu,
                                             bias=col("b1", layer(c) * FT + j)).then_inc(drained[b], 1)
                        if f is not None and j in (1, 2):
                            front_out(f, j - 1)
                if mid is not None:
                    if m is not None:
                        act.wait_ge(mixed, m + 1)
                    if mid > 0:
                        bw, kw = TURN["middle", mid - 1, 1]
                        act.wait_ge(filled[bw], kw + 1)
                    norm_w(1, mid, xhat, xr[:, mid % 4, :])
                if g is not None:
                    b, k = TURN["final features", g]
                    act.wait_ge(filled[b], k + 1)
                    if c is not None:
                        act.wait_ge(yn_lo_ready, c + 1)
                    elif final_of(n - 1) is not None:
                        act.wait_ge(fin_lo_ready, g)
                    nc.scalar.activation(yn[:, :], bank[b][:, :], ACT.Identity, bias=col("lnl_b"),
                                         scale=col("lnl_w")).then_inc(fin_hi_ready, 1)
                    if g >= BATCH:
                        last = TILES_PER_CHUNK * (g // BATCH - 1) + R * (g % BATCH) + R - 1
                        bw, kw = TURN["Wout", last, 1]
                        act.wait_ge(filled[bw], kw + 1)
                    nc.scalar.activation(fin_hi[:, g % BATCH, :], bank[b][:, :], ACT.Identity, bias=col("lnl_b"),
                                         scale=col("lnl_w")).then_inc(drained[b], 1)
                if w is not None:
                    act.wait_ge(offsets_ready, w + 1)
                    nc.scalar.activation(w_deq, offsets.rearrange("p i two -> p (i two)"), ACT.Identity,
                                         bias=minus_8_scales[:, w:w + 1], scale=col("scales", w)).then_inc(deq_ready, 1)
                if f == 1:
                    b, k = TURN["params",]
                    act.wait_ge(filled[b], k + 1)
                    nc.scalar.activation(par[:, :], bank[b][:, 0:NPAR], ACT.Copy).then_inc(drained[b], 1)
                    act.wait_ge(modulus_ready, 1)
                    nc.scalar.activation(decay[:, :], small[:, 2, :], ACT.Tanh).then_inc(decay_ready, 1)
                if mid is not None:
                    for u in range(2):
                        b, k = TURN["middle", mid, u]
                        act.wait_ge(filled[b], k + 1)
                        if mid >= 2 and u == 0:
                            bw, kw = TURN["back", mid - 2, 1]
                            act.wait_ge(filled[bw], kw + 1)
                        nc.scalar.activation(x_hi[:, mid % 2, u * KH:(u + 1) * KH, :].rearrange("p k t -> p (k t)"),
                                             bank[b][:, :], ACT.Copy).then_inc(x_hi_ready, 1)
                if w is not None:
                    for u in range(2):
                        b, k = TURN["weight", w, u]
                        act.wait_ge(filled[b], k + 1)
                        nc.scalar.activation(w_hi[:, u * KH:(u + 1) * KH, w * P:(w + 1) * P],
                                             bank[b][:, :].rearrange("p (k o) -> p k o", k=KH),
                                             ACT.Copy).then_inc(w_hi_ready, 1)
                for what, i in PREP.get(n, []):
                    b, k = TURN["prep", what, i]
                    act.wait_ge(filled[b], k + 1)
                    nc.scalar.activation(prep_to[what](i), bank[b][:, :], ACT.Copy).then_inc(
                        prep_hi_ready if (what, i) in SPLIT else drained[b], 1)
                if f is not None and f % 2 == 1:
                    i = f // R
                    b, k = TURN["Win", f // 2]
                    act.wait_ge(filled[b], k + 1)
                    if i >= BATCH:
                        act.wait_ge(mixed, STAGES_PER_CHUNK * (i // BATCH - 1) + i % BATCH + 1)
                    at = f % R // 2 * 2 * P
                    nc.scalar.activation(h_in[:, i % BATCH, at:at + 2 * P], bank[b][:, 0:2 * P], ACT.Identity,
                                         bias=col("bin")).then_inc(drained[b], 1)

        @block.vector
        def _(dve):
            steps = [0]

            def step(ins):
                steps[0] += 1
                ins.then_inc(vec_step, 1)
                return steps[0]

            def settle(count=None):
                dve.wait_ge(vec_step, steps[0] if count is None else count)

            vv = nc.vector

            def s(i):
                return small[:, i, :]

            def find_rotation():
                b, k = TURN["params",]
                dve.wait_ge(drained[b], k + 1)
                re, im = (par[:, PAR[q]:PAR[q] + LAYERS] for q in ("phz_re", "phz_im"))
                step(vv.tensor_tensor(s(3), re, re, ALU.mult))
                step(vv.tensor_tensor(s(4), im, im, ALU.mult))
                settle()
                step(vv.tensor_tensor(s(5), s(3), s(4), ALU.add))
                settle()
                vv.tensor_scalar(s(0), s(5), 1e-36, None, ALU.max).then_inc(modulus_squared, 1)
                step(vv.tensor_scalar(s(6), s(5), 1e-36, None, ALU.is_lt))
                dve.wait_ge(modulus_root, 1)
                settle()
                vv.tensor_tensor(s(2), s(5), s(1), ALU.mult).then_inc(modulus_ready, 1)
                step(vv.tensor_tensor(s(7), re, s(1), ALU.mult))
                step(vv.tensor_tensor(s(8), im, s(1), ALU.mult))
                step(vv.tensor_scalar(s(9), s(6), -1.0, 1.0, ALU.mult, ALU.add))
                settle()
                step(vv.tensor_tensor(s(7), s(7), s(9), ALU.mult))
                step(vv.tensor_tensor(s(8), s(8), s(9), ALU.mult))
                settle()
                step(vv.tensor_tensor(power[:, 0, 0, :], s(7), s(6), ALU.add))
                step(vv.tensor_scalar(power[:, 0, 1, :], s(8), -1.0, None, ALU.mult))
                settle()
                step(vv.tensor_tensor(s(10), power[:, 0, 0, :], power[:, 0, 0, :], ALU.mult))
                step(vv.tensor_tensor(s(11), power[:, 0, 1, :], power[:, 0, 1, :], ALU.mult))
                settle()
                step(vv.tensor_tensor(s(12), s(10), s(11), ALU.add))
                settle()
                step(vv.tensor_scalar(s(12), s(12), -0.5, 1.5, ALU.mult, ALU.add))
                settle()
                step(vv.tensor_tensor(power[:, 0, 0, :], power[:, 0, 0, :], s(12), ALU.mult))
                step(vv.tensor_tensor(power[:, 0, 1, :], power[:, 0, 1, :], s(12), ALU.mult))
                settle()
                lr, li = (par[:, PAR[q]:PAR[q] + LAYERS] for q in ("lc_re", "lc_im"))
                er, ei = power[:, 0, 0, :], power[:, 0, 1, :]
                step(vv.tensor_tensor(s(10), er, lr, ALU.mult))
                step(vv.tensor_tensor(s(11), ei, li, ALU.mult))
                step(vv.tensor_tensor(s(12), er, li, ALU.mult))
                step(vv.tensor_tensor(s(13), ei, lr, ALU.mult))
                settle()
                for st in range(BATCH):
                    step(vv.tensor_tensor(state[:, :, st, 0], s(10), s(11), ALU.add))
                    step(vv.tensor_tensor(state[:, :, st, 1], s(12), s(13), ALU.subtract))
                step(vv.memset(turn[:, :, 0, 0:1], 1.0))
                step(vv.memset(turn[:, :, 1, 0:1], 0.0))

                vv.tensor_scalar(minus_8_scales[:, :], par[:, PAR["scales"]:PAR["scales"] + OT], -8.0, None,
                                 ALU.mult).then_inc(modulus_ready, 1)

            def square(lev):
                cr, ci = power[:, lev, 0, :], power[:, lev, 1, :]
                step(vv.tensor_tensor(s(10), cr, cr, ALU.mult))
                step(vv.tensor_tensor(s(11), ci, ci, ALU.mult))
                step(vv.tensor_tensor(s(12), cr, ci, ALU.mult))
                settle()
                step(vv.tensor_tensor(s(13), s(10), s(11), ALU.subtract))
                step(vv.tensor_tensor(s(14), s(10), s(11), ALU.add))
                settle()
                step(vv.tensor_scalar(s(14), s(14), -1.0, 2.0, ALU.mult, ALU.add))
                settle()
                step(vv.tensor_tensor(power[:, lev + 1, 0, :], s(13), s(14), ALU.mult))
                step(vv.scalar_tensor_tensor(power[:, lev + 1, 1, :], s(12), 2.0, s(14), ALU.mult, ALU.mult))

            def double_table(lev, l0, l1):
                n, nl = 1 << lev, l1 - l0
                src = turn[:, l0:l1, :, 0:n]
                parts = [bout_rows[:, i * HALF:i * HALF + nl * 2 * n].rearrange("p (l c j) -> p l c j", l=nl, c=2) for i in range(2)]
                for i in range(2):
                    by = power[:, lev, i, l0:l1].rearrange("p (l c j) -> p l c j", c=1, j=1)
                    step(vv.tensor_tensor(parts[i], src, by.to_broadcast([P, nl, 2, n]), ALU.mult))
                settle()
                step(vv.tensor_tensor(turn[:, l0:l1, 0, n:2 * n], parts[0][:, :, 0, :], parts[1][:, :, 1, :],
                                      ALU.subtract))
                step(vv.tensor_tensor(turn[:, l0:l1, 1, n:2 * n], parts[0][:, :, 1, :], parts[1][:, :, 0, :],
                                      ALU.add))
                settle()

            def stats_w(i, tile, src):
                for u in range(2):
                    step(vv.bn_stats(bn_w[:, i, u, :], src[:, u * HALF:(u + 1) * HALF]))
                settle()
                step(vv.bn_aggr(mv_w[:, i, tile % 2, :], bn_w[:, i, :, :].rearrange("p a b -> p (a b)")))
                settle()
                vv.tensor_scalar(var_w[:, i, tile % 2:tile % 2 + 1], mv_w[:, i, tile % 2, 1:2], EPS, None, ALU.add).then_inc(var_w_ready[i], 1)

            def find_shift_w(i, tile):
                dve.wait_ge(rstd_w_ready[i], tile + 1)
                vv.scalar_tensor_tensor(shift_w[:, i, tile % 2:tile % 2 + 1], mv_w[:, i, tile % 2, 0:1], -1.0,
                                        rstd_w[:, i, tile % 2:tile % 2 + 1], ALU.mult, ALU.mult).then_inc(shift_w_ready[i], 1)

            def stats(i, q):
                b, k = TURN[TOKENS[i], q]
                dve.wait_ge(filled[b], k + 1)
                for r in range(R):
                    step(vv.bn_stats(bn[:, i, r, :], bank[b][:, r * P:(r + 1) * P]))
                settle()
                for r in range(R):
                    step(vv.bn_aggr(mv[:, i, r, :], bn[:, i, r, :]))
                settle()
                vv.tensor_scalar(var[:, i, :], mv[:, i, :, 1], EPS, None, ALU.add).then_inc(var_ready[i], 1)

            def find_shift(i, q):
                dve.wait_ge(rstd_ready[i], q + 1)
                vv.scalar_tensor_tensor(shift[:, i, :], mv[:, i, :, 0], -1.0, rstd[:, i, :], ALU.mult,
                                        ALU.mult).then_inc(shift_ready[i], 1)

            def residual(key, u, t):
                b, k = TURN[key, t, u]
                dve.wait_ge(filled[b], k + 1)
                at = xr[:, t % 4, u * HALF:(u + 1) * HALF]
                vv.tensor_tensor(at, bank[b][:, :], at, ALU.add).then_inc(drained[b], 1)

            for n in SLOTS:
                m, c, g = mixer_of(n), mlp_of(n), final_of(n)
                f, mid, bk, w = front_of(n), middle_of(n), back_of(n), weight_of(n)
                if c is not None:
                    stats(1, c)
                before = middle_of(n - 1)
                if before is not None:
                    for u in range(2):
                        b, k = TURN["middle", before, u]
                        dve.wait_ge(x_hi_ready, 2 * before + u + 1)
                        at = slice(u * KH, (u + 1) * KH)
                        vv.tensor_tensor(x_lo[:, before % 2, at, :].rearrange("p k t -> p (k t)"), bank[b][:, :],
                                         x_hi[:, before % 2, at, :].rearrange("p k t -> p (k t)").bitcast(fp32),
                                         ALU.subtract).then_inc(drained[b], 1)
                if c is not None:
                    find_shift(1, c)
                if m is not None:
                    stats(0, m)
                before = back_of(n - 1)
                if before is not None:
                    residual("back", 1, before)
                if m is not None:
                    find_shift(0, m)
                before = weight_of(n - 1)
                if before is not None:
                    for u in range(2):
                        b, k = TURN["weight", before, u]
                        dve.wait_ge(w_hi_ready, 2 * before + u + 1)
                        at, cols = slice(u * KH, (u + 1) * KH), slice(before * P, (before + 1) * P)
                        vv.tensor_tensor(w_lo[:, at, cols], bank[b][:, :].rearrange("p (k o) -> p k o", k=KH),
                                         w_hi[:, at, cols].bitcast(fp32), ALU.subtract).then_inc(drained[b], 1)
                if g is not None:
                    stats(2, g)
                for q in front_stats(f):
                    if q < 4:
                        dve.wait_ge(x_first_loaded[q], 16)
                    else:
                        dve.wait_ge(x_loaded[q % 2], 16 * (q // 2 - 1))
                    stats_w(0, q, front_buffer(q))
                if g is not None:
                    find_shift(2, g)
                if f is not None:
                    find_shift_w(0, f)
                if mid is not None:
                    dve.wait_ge(xr_biased, mid + 1)
                    residual("Wout", 0, mid)
                    residual("Wout", 1, mid)
                    b, k = TURN["Wout", mid, 1]
                    dve.wait_ge(drained[b], k + 1)
                    stats_w(1, mid, xr[:, mid % 4, :])
                if f == 1:
                    find_rotation()
                if f is not None and 2 <= f <= 4:
                    settle()
                    for lev in range((f - 2) * (LEVELS // 3), (f - 1) * (LEVELS // 3)):
                        square(lev)
                        settle()
                        if lev < SHARED_LEVELS:
                            double_table(lev, 0, LAYERS)
                if f == 5:
                    for lev in range(SHARED_LEVELS, LEVELS):
                        double_table(lev, 0, 1)
                if w is not None:
                    dve.wait_ge(w_loaded[w % 2], 32 * (w // 2 + 1))
                    nib = nibbles_in[w % 2]
                    if w > 0:
                        dve.wait_ge(w_ready, w)
                    vv.tensor_scalar(offsets[:, :, 0], nib, 15, None, ALU.bitwise_and)
                    vv.tensor_scalar(offsets[:, :, 1], nib, 4, 15, ALU.logical_shift_right,
                                     ALU.bitwise_and).then_inc(offsets_ready, 1)
                if c is not None:
                    dve.wait_ge(yn_hi_ready, c + 1)
                    b, k = TURN["mlp features", c]
                    dve.wait_ge(drained[b], k + 1)
                    if c > 0:
                        b, k = TURN["W1", c - 1, FT - 1]
                        dve.wait_ge(filled[b], k + 1)
                    vv.tensor_tensor(yn_lo[:, :], yn[:, :], yn_hi[:, :].bitcast(fp32),
                                     ALU.subtract).then_inc(yn_lo_ready, 1)
                if m is not None:
                    l, st = layer(m), stream(m)
                    b, k = TURN["mixer features", m]
                    dve.wait_ge(drained[b], k + 1)
                    if m == 0:
                        dve.wait_ge(decay_ready, 1)
                    if mid is not None and mid > 0:
                        b, k = TURN["middle", mid - 1, 1]
                        dve.wait_ge(filled[b], k + 1)
                    for part in range(2):
                        vv.tensor_tensor(z[:, part, :], y[:, :], turn[:, l, part, :], ALU.mult).then_inc(y_rotated, 1)
                if m is not None:
                    scans = []
                    for part in range(2):
                        dve.wait_ge(y_rotated, 2 * m + part + 1)
                        scans.append(step(vv.tensor_tensor_scan(
                            z[:, part, :], decay[:, l:l + 1].to_broadcast([P, CHUNK]), z[:, part, :],
                            state[:, l, st, part:part + 1], ALU.mult, ALU.add)))
                if m is not None:
                    settle(scans[1])
                    cr, ci = power[:, LEVELS, 0, l:l + 1], power[:, LEVELS, 1, l:l + 1]
                    z0, z1 = z[:, 0, CHUNK - 1:CHUNK], z[:, 1, CHUNK - 1:CHUNK]
                    step(vv.tensor_tensor(s(10)[:, 0:1], z1, ci, ALU.mult))
                    step(vv.tensor_tensor(s(11)[:, 0:1], z0, ci, ALU.mult))
                    step(vv.tensor_tensor(s(12)[:, 0:1], z0, cr, ALU.mult))
                    first = step(vv.tensor_tensor(s(13)[:, 0:1], z1, cr, ALU.mult))
                    settle(first)
                    back = [step(vv.tensor_tensor(z[:, part, :], z[:, part, :], turn[:, l, part, :], ALU.mult))
                            for part in range(2)]
                    step(vv.tensor_tensor(state[:, l, st, 0:1], s(12)[:, 0:1], s(10)[:, 0:1], ALU.add))
                    step(vv.tensor_tensor(state[:, l, st, 1:2], s(13)[:, 0:1], s(11)[:, 0:1], ALU.subtract))
                    src = h_in if l == 0 else h
                    if l > 0:
                        b, k = TURN["W2", m - BATCH]
                        dve.wait_ge(drained[b], k + 1)
                    settle(back[0])
                    step(vv.scalar_tensor_tensor(h[:, st, :], z[:, 0, :], col("scl", l), src[:, st, :],
                                                 ALU.mult, ALU.add))
                    settle()
                    vv.scalar_tensor_tensor(h[:, st, :], z[:, 1, :], col("scl", l), h[:, st, :],
                                            ALU.mult, ALU.add).then_inc(mixed, 1)
                if mid is not None:
                    find_shift_w(1, mid)
                if bk is not None:
                    residual("back", 0, bk)
                if 0 <= n < LAYERS - 1:
                    for lev in range(SHARED_LEVELS, LEVELS):
                        double_table(lev, n + 1, n + 2)
                    if n == LAYERS - 2:
                        vv.memset(small[:, 15, :], 0.0).then_inc(tables_ready, 1)
                if c is not None:
                    b, k = TURN["W2", c]
                    dve.wait_ge(filled[b], k + 1)
                    dve.wait_ge(mixed, c + 1)
                    vv.scalar_tensor_tensor(h[:, stream(c), :], bank[b][:, :], col("b2", layer(c)),
                                            h[:, stream(c), :], ALU.add, ALU.add).then_inc(drained[b], 1)
                if g is not None:
                    b, k = TURN["final features", g]
                    dve.wait_ge(drained[b], k + 1)
                    dve.wait_ge(fin_hi_ready, g + 1)
                    vv.tensor_tensor(fin_lo[:, g % BATCH, :], yn[:, :], fin_hi[:, g % BATCH, :].bitcast(fp32),
                                     ALU.subtract).then_inc(fin_lo_ready, 1)
                for what, i in PREP.get(n, []):
                    if (what, i) in SPLIT:
                        b, k = TURN["prep", what, i]
                        dve.wait_ge(prep_hi_ready, SPLIT.index((what, i)) + 1)
                        cols = slice(i * HALF, (i + 1) * HALF)
                        hi, lo = ((W1_hi[:, i, :], W1_lo[:, i, :]) if what == "W1" else
                                  (Wout_hi[:, cols], Wout_lo[:, cols]))
                        vv.tensor_tensor(lo, bank[b][:, :], hi.bitcast(fp32), ALU.subtract).then_inc(drained[b], 1)

        @block.tensor
        def _(pe):
            mm, tr = nc.tensor.matmul, nc.tensor.transpose

            def claim(*key):
                b, k = TURN[key]
                if k > 0:
                    pe.wait_ge(drained[b], k)
                return bank[b], filled[b]

            def drained_of(*key):
                b, k = TURN[key]
                pe.wait_ge(drained[b], k + 1)

            pe.wait_ge(ident_ready, 1)

            def to_tokens(key, src):
                ps, full = claim(*key)
                for r in range(R):
                    last = tr(ps[:, r * P:(r + 1) * P], src[:, r * P:(r + 1) * P], ident[:, :])
                last.then_inc(full, 1)

            def to_features(key, lane, token_key):
                ps, full = claim(*key)
                drained_of(*token_key)
                for r in range(R):
                    last = tr(ps[:, r * P:(r + 1) * P], normed[:, lane, r, :], ident[:, :])
                last.then_inc(full, 1)

            def width_transpose(key, src, u):
                ps, full = claim(*key)
                for i in range(KH):
                    q = u * KH + i
                    last = tr(ps[:, i * P:(i + 1) * P], src[:, q * P:(q + 1) * P], ident[:, :])
                last.then_inc(full, 1)

            def three_pass(ps, hi, lo, w_h, w_l, first, last):
                mm(ps, hi, w_h, start=first, stop=False)
                mm(ps, hi, w_l, start=False, stop=False)
                return mm(ps, lo, w_h, start=False, stop=last)

            def big(bk, u, q0, q1):
                b, k = TURN["back", bk, u]
                cols = slice(u * HALF, (u + 1) * HALF)
                if q0 == 0:
                    claim("back", bk, u)
                for q in range(q0, q1):
                    last = three_pass(bank[b][:, :], x_hi[:, bk % 2, q, :], x_lo[:, bk % 2, q, :], w_hi[:, q, cols], w_lo[:, q, cols],
                                      q == 0, q == K - 1)
                if q1 == K:
                    last.then_inc(filled[b], 1)

            def wout(mid, u):
                ps, full = claim("Wout", mid, u)
                st, r = mid % TILES_PER_CHUNK // R, mid % R
                at, cols = slice(r * P, (r + 1) * P), slice(u * HALF, (u + 1) * HALF)
                pe.wait_ge(fin_lo_ready, BATCH * (mid // TILES_PER_CHUNK) + st + 1)
                three_pass(ps[:, :], fin_hi[:, st, at], fin_lo[:, st, at], Wout_hi[:, cols], Wout_lo[:, cols],
                           True, True).then_inc(full, 1)

            nat = {"Win": lambda i, q: Win_nat[:, (i * KH + q) * P:(i * KH + q + 1) * P],
                   "W1": lambda i, q: W1_nat[:, i, q, :], "W2": lambda i, q: W2_nat[:, i, q * P:(q + 1) * P],
                   "Wout": lambda i, q: Wout_nat[:, i * KH + q, :]}

            for n in SLOTS:
                m, c, g = mixer_of(n), mlp_of(n), final_of(n)
                f, mid, bk, w = front_of(n), middle_of(n), back_of(n), weight_of(n)
                if g is not None:
                    drained_of("W2", n - BATCH)
                    to_tokens(("final tokens", g), h[:, g % BATCH, :])
                if bk is not None:
                    drained_of("middle", bk, 0)
                    drained_of("middle", bk, 1)
                    if bk == 0:
                        drained_of("weight", OT - 1, 0)
                        drained_of("weight", OT - 1, 1)
                    big(bk, 0, 0, KH)
                if c is not None:
                    to_features(("mlp features", c), 1, ("mlp tokens", c))
                if mid is not None:
                    wout(mid, 0)
                    wout(mid, 1)
                if m is not None:
                    to_features(("mixer features", m), 0, ("mixer tokens", m))
                if bk is not None:
                    big(bk, 0, KH, K)
                    big(bk, 1, 0, KH)

                def front_in():
                    pe.wait_ge(xhat_ready[0], f + 1)
                    width_transpose(("front", f, 0), front_buffer(f), 0)
                    width_transpose(("front", f, 1), front_buffer(f), 1)

                if c is not None:
                    pe.wait_ge(yn_hi_ready, c + 1)

                    def mlp_in(j):
                        ps, full = claim("W1", c, j)
                        at = slice(j * P, (j + 1) * P)
                        mm(ps[:, :], W1_hi[:, layer(c), at], yn_hi[:, :], start=True, stop=False)
                        mm(ps[:, :], W1_lo[:, layer(c), at], yn_hi[:, :], start=False, stop=False)
                        if j == 0:
                            pe.wait_ge(yn_lo_ready, c + 1)
                        mm(ps[:, :], W1_hi[:, layer(c), at], yn_lo[:, :], start=False, stop=True).then_inc(full, 1)

                    mlp_in(0)
                    mlp_in(1)
                    if f is not None:
                        front_in()
                    b, k = TURN["W2", c]
                    claim("W2", c)
                    for j in range(FT):
                        drained_of("W1", c, j)
                        mm(bank[b][:, :], W2T[:, layer(c), j, :], ff[:, j % 2, :], start=(j == 0),
                           stop=(j == FT - 1)).then_inc(ff_used if j < FT - 1 else filled[b], 1)
                        if j + 2 < FT:
                            mlp_in(j + 2)
                elif f is not None:
                    front_in()
                if mlp_of(n + 1) is not None:
                    pe.wait_ge(mixed, mlp_of(n + 1) + 1)
                    to_tokens(("mlp tokens", mlp_of(n + 1)), h[:, stream(n), :])
                if g is not None:
                    to_features(("final features", g), 1, ("final tokens", g))
                if mid is not None:
                    pe.wait_ge(xhat_ready[1], mid + 1)
                    for u in range(2):
                        width_transpose(("middle", mid, u), xhat, u)
                next_m = mixer_of(n + 1)
                if next_m is not None:
                    if layer(next_m) == 0:
                        drained_of("Win", 2 * (BATCH * (next_m // STAGES_PER_CHUNK) + stream(next_m)) + 1)
                        to_tokens(("mixer tokens", next_m), h_in[:, stream(next_m), :])
                    else:
                        drained_of("W2", next_m - BATCH)
                        to_tokens(("mixer tokens", next_m), h[:, stream(next_m), :])
                if bk is not None:
                    big(bk, 1, KH, K)
                if f == 1:
                    pe.wait_ge(params_loaded, 16 * len(vectors))
                    ps, full = claim("params")
                    tr(ps[:, 0:NPAR], par_rows, ident[0:NPAR, 0:NPAR]).then_inc(full, 1)
                if w is not None:
                    pe.wait_ge(w_ready, w + 1)
                    for u in range(2):
                        width_transpose(("weight", w, u), w_nat[w % 2], u)
                for what, i in PREP.get(n, []):
                    pe.wait_ge(nat_loaded[what], 16)
                    ps, full = claim("prep", what, i)
                    for q in range(KH):
                        last = tr(ps[:, q * P:(q + 1) * P], nat[what](i, q), ident[:, :])
                    last.then_inc(full, 1)
                if f is not None and f % 2 == 1:
                    drained_of("prep", "Win", 0)
                    drained_of("prep", "Win", 1)
                    drained_of("front", f, 0)
                    drained_of("front", f, 1)
                    ps, full = claim("Win", f // 2)
                    for q in range(K):
                        last = mm(ps[:, 0:2 * P], WinT[:, q, :], xT[:, q, :], start=(q == 0), stop=(q == K - 1))
                    last.then_inc(full, 1)


def kernel(**inputs):
    import numpy as _np
    import concourse.bacc as _bacc
    from concourse import mybir as _mybir
    from concourse.bass_utils import run_bass_kernel_spmd as _run

    nc = _bacc.Bacc("TRN2", target_bir_lowering=False, num_devices=1)
    arrays, args = {}, []
    for name in _INS:
        a = _np.ascontiguousarray(inputs[name])
        arrays[f"in_{name}_dram"] = a
        args.append(nc.dram_tensor(f"in_{name}_dram", a.shape, _mybir.dt.from_np(a.dtype), kind="ExternalInput").ap())
    for i, (shape, dtype) in enumerate(_OUTS):
        dt = _mybir.dt.from_np(_np.dtype(dtype))
        args.append(nc.dram_tensor(f"out_{i}_dram", shape, dt, kind="ExternalOutput").ap())
    sequence_block(nc, *args)
    r = _run(nc, [arrays], core_ids=[0])
    got = tuple(r.results[0][f"out_{i}_dram"] for i in range(len(_OUTS)))
    return got[0]
```

```python
import concourse.bass as bass
from concourse import mybir
from contextlib import ExitStack

_INS = ['L0_attn_x', 'L0_attn_Win', 'L0_attn_bin', 'L0_attn_ln1_w', 'L0_attn_ln1_b', 'L0_attn_phz_re',
        'L0_attn_phz_im', 'L0_attn_lc_re', 'L0_attn_lc_im', 'L0_attn_sc_lin', 'L0_attn_ln2_w', 'L0_attn_ln2_b',
        'L0_attn_W1', 'L0_attn_b1', 'L0_attn_W2', 'L0_attn_b2', 'L0_attn_lnl_w', 'L0_attn_lnl_b',
        'L0_attn_Wout', 'L0_attn_bout', 'L0_ffn_base_packed', 'L0_ffn_scales', 'L0_ffn_w_ortho']
_OUTS = [((2, 2048, 1024), 'float32')]


def sequence_block(nc, x, Win, bin_, ln1_w, ln1_b, phz_re, phz_im, lc_re, lc_im, sc_lin, ln2_w, ln2_b,
                   W1, b1, W2, b2, lnl_w, lnl_b, Wout, bout, packed, scales, ortho, out):
    fp32, f32r, i32 = mybir.dt.float32, mybir.dt.float32r, mybir.dt.int32
    ALU, ACT = mybir.AluOpType, mybir.ActivationFunctionType
    EPS = 1e-5

    P = nc.NUM_PARTITIONS
    BATCH, LEN, V = x.shape
    LAYERS, FF, D = W1.shape
    CHUNK = 512
    R = CHUNK // P
    CHUNKS = LEN // CHUNK
    STAGES_PER_CHUNK = LAYERS * BATCH
    TILES_PER_CHUNK = R * BATCH
    STAGES = CHUNKS * STAGES_PER_CHUNK
    TILES = CHUNKS * TILES_PER_CHUNK
    K = V // P
    KH = K // 2
    HALF = V // 2
    FT = FF // P
    OT = ortho.shape[0] // P
    AHEAD = R
    MID, BACK = STAGES_PER_CHUNK + 1, STAGES_PER_CHUNK + 2
    assert STAGES_PER_CHUNK == TILES_PER_CHUNK == OT and BATCH == 2 and D == P

    SLOTS = range(-AHEAD, TILES + BACK + 1)

    def mixer_of(n):
        return n if 0 <= n < STAGES else None

    def mlp_of(n):
        return n - 1 if 0 <= n - 1 < STAGES else None

    def final_of(n):
        chunk, s = n // STAGES_PER_CHUNK - 1, n % STAGES_PER_CHUNK
        return BATCH * chunk + s if s < BATCH and 0 <= chunk < CHUNKS else None

    def fronts_of(n):
        tiles = ([n + AHEAD] if n < 0 else range(R, TILES_PER_CHUNK) if n == 0 else
                 range(TILES_PER_CHUNK, TILES_PER_CHUNK + 2) if n == 1 else [n + TILES_PER_CHUNK])
        return [f for f in tiles if f < TILES]

    def win_of(n):
        done = fronts_of(n - 1) if n > 1 else []
        return done[-1] // 2 if done and done[-1] % 2 == 1 else None

    def middle_of(n):
        return n - MID if 0 <= n - MID < TILES else None

    def back_of(n):
        return n - BACK if 0 <= n - BACK < TILES else None

    def weight_of(n):
        return n - 1 if 0 <= n - 1 < OT else None

    def layer(stage):
        return stage % STAGES_PER_CHUNK // BATCH

    def stream(stage):
        return stage % BATCH

    def rows(dram, tile):
        chunk, g = divmod(tile, TILES_PER_CHUNK)
        first = chunk * CHUNK + g % R * P
        return dram[g // R, first:first + P, :]

    def filling(n):
        return mlp_of(n) is not None and n < BACK

    PREP = {-4: [("Win", 0), ("Win", 1)], -2: [("Wout", 0), ("Wout", 1)], -1: [("W1", 0), ("W1", 1)],
            0: [("W1", 2), ("W1", 3)] + [("W2", l) for l in range(LAYERS)]}

    A_TOK, C_TOK, FEAT, FF0, FF1, ACC, PAIR0, PAIR1 = range(8)
    TURN, turns = {}, [0] * 8

    def take(bank, key):
        TURN[key] = (bank, turns[bank])
        turns[bank] += 1
    take(PAIR1, ("params", 0))
    for n in SLOTS:
        m, c, g = mixer_of(n), mlp_of(n), final_of(n)
        mid, bk, w = middle_of(n), back_of(n), weight_of(n)
        if m is not None:
            take(A_TOK, ("mixer tokens", m))
        if c is not None:
            take(C_TOK, ("mlp tokens", c))
        if g is not None:
            take(C_TOK if filling(n) else FF0, ("final tokens", g))
        if bk is not None:
            take(PAIR0, ("back", bk, 0))
        if c is not None:
            take(FF1, ("mlp features", c))
        if win_of(n) is not None and filling(n):
            take(ACC, ("Win", win_of(n)))
        if mid is not None:
            take(PAIR1, ("Wout", mid, 0))
            take(ACC, ("Wout", mid, 1))
        if m is not None and n > 0:
            take(FEAT, ("mixer features", m))
        if bk is not None:
            take(PAIR1, ("back", bk, 1))
        if win_of(n) is not None and not filling(n):
            take(ACC, ("Win", win_of(n)))
        if c is not None:
            for j in range(FT):
                take((FF0, FF1)[j % 2], ("W1", c, j))
            take(ACC, ("W2", c))
        for f in fronts_of(n):
            take(FF0 if n == 0 else A_TOK, ("front", f, 0))
            take(FEAT, ("front", f, 1))
            if n <= 0 and f % 2 == 1:
                take(ACC, ("Win", f // 2))
            if f == R:
                take(FEAT, ("mixer features", 0))
            if f == 1:
                take(PAIR1, ("params", 1))
        if w is not None:
            take(PAIR0, ("weight", w, 0))
            take(PAIR1, ("weight", w, 1))
        if g is not None:
            take(FEAT, ("final features", g))
        if mid is not None:
            take(FF0, ("middle", mid, 0))
            take(FF1, ("middle", mid, 1))
        for i, what in enumerate(PREP.get(n, [])):
            take((PAIR0, PAIR1, FF0, FF1, FF0, FF1)[i], ("prep",) + what)

    vectors = [("phz_re", phz_re), ("phz_im", phz_im), ("lc_re", lc_re), ("lc_im", lc_im),
               ("bin", bin_.rearrange("(a d) -> a d", a=1)), ("ln1_w", ln1_w), ("ln1_b", ln1_b),
               ("scl", sc_lin), ("ln2_w", ln2_w), ("ln2_b", ln2_b),
               ("b1", b1.rearrange("l (j p) -> (l j) p", p=P)), ("b2", b2),
               ("lnl_w", lnl_w.rearrange("(a d) -> a d", a=1)),
               ("lnl_b", lnl_b.rearrange("(a d) -> a d", a=1)),
               ("scales", scales.rearrange("(t p) a -> (t a) p", p=P))]
    FIRST = 4
    PAR, NPAR = {}, 0
    for name, v in vectors:
        PAR[name] = NPAR
        NPAR += v.shape[0]
    PAR_FIRST = FIRST * LAYERS

    with ExitStack() as ctx:
        def sb(name, shape, dt=fp32):
            return ctx.enter_context(nc.sbuf_tensor(name, shape, dt))

        def sem(name):
            return ctx.enter_context(nc.semaphore(name))

        ident = sb("ident", [P, P])
        minus_half = sb("minus_half", [P, R])
        two = sb("two", [P, LAYERS])
        par = sb("par", [P, NPAR])
        bout_rows = sb("bout_rows", [P, V])
        WinT = sb("WinT", [P, K, P])
        W1_hi = sb("W1_hi", [P, LAYERS, FF], f32r)
        W1_lo = sb("W1_lo", [P, LAYERS, FF], f32r)
        W2T = sb("W2T", [P, LAYERS, FT, P])
        Wout_hi = sb("Wout_hi", [P, V], f32r)
        Wout_lo = sb("Wout_lo", [P, V], f32r)
        w_hi = sb("w_hi", [P, K, V], f32r)
        w_lo = sb("w_lo", [P, K, V], f32r)
        LEVELS = CHUNK.bit_length() - 1
        SHARED_LEVELS = 6
        POWER_STEPS, TABLE_STEPS = 9, 4
        SQUARES = {-3: range(0, 2), -2: range(2, 5), -1: range(5, LEVELS)}
        DOUBLINGS = {-2: range(0, 2), -1: range(2, 6), 0: range(6, LEVELS)}
        turn = sb("turn", [P, LAYERS, 2, CHUNK])
        power = sb("power", [P, LEVELS + 1, 2, LAYERS])
        decay = sb("decay", [P, LAYERS])
        state = sb("state", [P, LAYERS, BATCH, 2])
        small = sb("small", [P, 14, LAYERS])
        pool_small = sb("pool_small", [P, 7, LAYERS])
        xin = sb("xin", [P, 2, V])
        xT = sb("xT", [P, K, 2 * P])
        xr = sb("xr", [P, 4, V])
        x_hi = sb("x_hi", [P, 2, K, P], f32r)
        x_lo = sb("x_lo", [P, 2, K, P], f32r)
        h_in = sb("h_in", [P, BATCH, CHUNK])
        h = sb("h", [P, BATCH, CHUNK])
        fin_hi = sb("fin_hi", [P, BATCH, CHUNK], f32r)
        fin_lo = sb("fin_lo", [P, BATCH, CHUNK], f32r)
        normed = sb("normed", [P, 2, R, P])
        y = sb("y", [P, CHUNK])
        z = sb("z", [P, 2, CHUNK])
        yn = sb("yn", [P, CHUNK])
        yn_hi = sb("yn_hi", [P, CHUNK], f32r)
        yn_lo = sb("yn_lo", [P, CHUNK], f32r)
        ff = sb("ff", [P, 2, CHUNK])
        bn = sb("bn", [P, 3, R, 6])
        mv = sb("mv", [P, 3, R, 2])
        var = sb("var", [P, 3, R])
        rstd = sb("rstd", [P, 3, R])
        shift = sb("shift", [P, 3, R])
        bn_w = sb("bn_w", [P, 2, 2, 6])
        mv_w = sb("mv_w", [P, 2, 2, 2])
        var_w = sb("var_w", [P, 2, 2])
        rstd_w = sb("rstd_w", [P, 2, 2])
        shift_w = sb("shift_w", [P, 2, 2])
        par_rows = h[0:NPAR, 0, 0:P]
        xr_flat = xr[:, :, :].rearrange("p a v -> p (a v)")
        W1_nat = xr_flat[:, 0:2 * V].rearrange("p (l j d) -> p l j d", l=LAYERS, j=FT)
        W2_nat = xr_flat[:, 2 * V:4 * V].rearrange("p (l f) -> p l f", l=LAYERS)
        Win_nat = z[:, :, :].rearrange("p a t -> p (a t)")
        Wout_nat = normed[:, :, :, :].rearrange("p a r d -> p (a r) d")
        w_nat = [xr[:, 0, :], xr[:, 1, :]]
        nibbles_in = [xr[:, 2, i * HALF:(i + 1) * HALF].bitcast(i32) for i in range(2)]
        offsets = xr[:, 3, :].bitcast(i32).rearrange("p (i two) -> p i two", two=2)
        w_deq = xr[:, 3, :]
        double_early = W2T[:, LAYERS // 2:LAYERS, :, :].rearrange("p l j d -> p (l j d)")
        xhat = z[:, :, :].rearrange("p a t -> p (a t)")
        minus_8_scales = sb("minus_8_scales", [P, OT])

        bank = [ctx.enter_context(nc.psum_tensor(f"bank{i}", [P, CHUNK], fp32)) for i in range(8)]
        filled = [sem(f"bank{i}_filled") for i in range(8)]
        drained = [sem(f"bank{i}_drained") for i in range(8)]

        params_loaded, bout_loaded = [sem(f"params_loaded{i}") for i in range(2)], sem("bout_loaded")
        nat_loaded = {k: sem(f"{k}_loaded") for k in ("Win", "W1", "W2", "Wout")}
        x_loaded = [sem(f"x_loaded{i}") for i in range(2)]
        x_first_loaded = [sem(f"x_first_loaded{i}") for i in range(TILES_PER_CHUNK)]
        xr_loaded = [sem(f"xr_loaded{i}") for i in range(4)]
        w_loaded = [sem(f"w_loaded{i}") for i in range(2)]
        stored = [sem(f"stored{i}") for i in range(4)]
        ident_zeroed, ident_ready = sem("ident_zeroed"), sem("ident_ready")
        par_ready, modulus_squared, modulus_root = sem("par_ready"), sem("modulus_squared"), sem("modulus_root")
        modulus_ready, decay_ready = sem("modulus_ready"), sem("decay_ready")
        var_ready = [sem(f"var_ready{i}") for i in range(3)]
        rstd_ready = [sem(f"rstd_ready{i}") for i in range(3)]
        shift_ready = [sem(f"shift_ready{i}") for i in range(3)]
        y_rotated, mixed = sem("y_rotated"), sem("mixed")
        yn_hi_ready, yn_lo_ready, fin_hi_ready, fin_lo_ready = (
            sem(q) for q in ("yn_hi_ready", "yn_lo_ready", "fin_hi_ready", "fin_lo_ready"))
        ff_used = sem("ff_used")
        rotation_ready, power_step = sem("rotation_ready"), sem("power_step")
        tables_shared, table_step = sem("tables_shared"), sem("table_step")
        prep_hi_ready, offsets_ready, deq_ready = sem("prep_hi_ready"), sem("offsets_ready"), sem("deq_ready")
        var_w_ready = [sem(f"var_w_ready{i}") for i in range(2)]
        rstd_w_ready = [sem(f"rstd_w_ready{i}") for i in range(2)]
        shift_w_ready = [sem(f"shift_w_ready{i}") for i in range(2)]
        xhat_ready = [sem(f"xhat_ready{i}") for i in range(2)]
        xr_biased = sem("xr_biased")
        x_hi_ready = sem("x_hi_ready")
        w_ready, w_hi_ready = sem("w_ready"), sem("w_hi_ready")
        vec_step = sem("vec_step")

        def front_buffer(t):
            if t < TILES_PER_CHUNK:
                return [xr[:, 0, :], xr[:, 1, :], xr[:, 2, :], xr[:, 3, :], xin[:, 0, :], xin[:, 1, :],
                        ff[:, :, :].rearrange("p a t -> p (a t)"), bout_rows[:, :]][t]
            return xin[:, t % 2, :]

        def col(name, i=0):
            return par[:, PAR[name] + i:PAR[name] + i + 1]

        TOKENS = ["mixer tokens", "mlp tokens", "final tokens"]
        FEATURES = ["mixer features", "mlp features", "final features"]

        def after(f):
            return [q for q in ((0, 1) if f == 0 else (f + 1,)) if q < TILES]

        EARLY = {n: [n + AHEAD + 2] for n in range(1 - AHEAD, 1)}
        EARLY[-AHEAD] = [0, 1]

        def lane_freed(engine, i, q, n):
            lane = min(i, 1)
            last = (FEATURES[i], q - 1)
            if i == 2 and mlp_of(n) is not None:
                last = ("mlp features", mlp_of(n))
            elif i == 1 and final_of(n - 1) is not None:
                last = ("final features", final_of(n - 1))
            if last in TURN:
                b, k = TURN[last]
                engine.wait_ge(filled[b], k + 1)
            return lane

        def shifts(i, q):
            return sum(i > 0 or not filling(stage) for stage in range(q + 1))

        SPLIT = [q for n in sorted(PREP) for q in PREP[n] if q[0] in ("W1", "Wout")]

        block = ctx.enter_context(nc.Block())

        @block.sync
        def _(sp):
            for t in range(TILES_PER_CHUNK):
                sp.dma_start(front_buffer(t), rows(x, t)).then_inc(x_first_loaded[t], 16)
                if t == 3:
                    sp.dma_start(Win_nat, Win).then_inc(nat_loaded["Win"], 16)
                    for name, v in vectors[len(vectors) // 2:]:
                        sp.dma_start(par_rows[PAR[name]:PAR[name] + v.shape[0], :], v).then_inc(params_loaded[1], 16)
                    sp.dma_start(Wout_nat, Wout.rearrange("(j p) d -> p j d", p=P)).then_inc(nat_loaded["Wout"], 16)

            def load_weight(t):
                if t < OT:
                    sp.dma_start(w_nat[t % 2], ortho[t * P:(t + 1) * P, :]).then_inc(w_loaded[t % 2], 16)
                    sp.dma_start(nibbles_in[t % 2], packed[t * P:(t + 1) * P, :]).then_inc(w_loaded[t % 2], 16)

            def load_middle(t):
                if 0 <= t < TILES:
                    if t < 4:
                        b, k = TURN["weight", OT - 1 if t else OT - 2, 1]
                        sp.wait_ge(filled[b], k + 1)
                    else:
                        sp.wait_ge(stored[t % 4], 16 * (t // 4))
                    sp.dma_start(xr[:, t % 4, :], rows(x, t)).then_inc(xr_loaded[t % 4], 16)

            for n in SLOTS:
                if n == 1:
                    for i in range(LAYERS - 2, LAYERS):
                        b, k = TURN["prep", "W2", i]
                        sp.wait_ge(filled[b], k + 1)
                    load_weight(0)
                    load_weight(1)
                bk, w = back_of(n), weight_of(n)
                for f in fronts_of(n):
                    if f == 1 or f == 3:
                        b, k = TURN["front", f, 1]
                        sp.wait_ge(filled[b], k + 1)
                        if f == 1:
                            sp.dma_start(W1_nat, W1.rearrange("l (j p) d -> p l j d", p=P)).then_inc(nat_loaded["W1"], 16)
                        else:
                            sp.dma_start(W2_nat, W2.rearrange("l d f -> d l f")).then_inc(nat_loaded["W2"], 16)
                    q = f + 4 if f < 6 else f + 2
                    if f in (4, 5) or 8 <= q - 2 and q < TILES:
                        b, k = TURN["front", f, 1]
                        sp.wait_ge(filled[b], k + 1)
                        sp.dma_start(front_buffer(q), rows(x, q)).then_inc(x_loaded[q % 2], 16)
                if w is not None:
                    b, k = TURN["weight", w, 1]
                    sp.wait_ge(filled[b], k + 1)
                    load_weight(w + 2)
                if bk is not None:
                    b, k = TURN["back", bk, 1]
                    sp.wait_ge(drained[b], k + 1)
                    sp.dma_start(rows(out, bk), xr[:, bk % 4, :]).then_inc(stored[bk % 4], 16)
                if n == 2 * (LAYERS - 1):
                    sp.wait_ge(table_step, TABLE_STEPS * (LEVELS - SHARED_LEVELS) * (LAYERS - 1))
                    sp.dma_start(bout_rows[:, :], bout.rearrange("(a v) -> a v", a=1).to_broadcast([P, V])).then_inc(bout_loaded, 16)
                load_middle(n - MID + 2)
            for i in range(4):
                sp.wait_ge(stored[i], 16 * (TILES // 4))

        @block.gpsimd
        def _(pool):
            nc.gpsimd.memset(ident[:, :], 0.0).then_inc(ident_zeroed, 1)
            nc.gpsimd.memset(minus_half[:, :], -0.5).then_inc(ident_zeroed, 1)
            nc.gpsimd.memset(two[:, :], 2.0).then_inc(ident_zeroed, 1)
            pool.wait_ge(ident_zeroed, 3)
            nc.gpsimd.affine_select(out=ident[:, :], in_=ident[:, :], compare_op=ALU.not_equal, fill=1.0, base=0,
                                    pattern=[[-1, P]], channel_multiplier=1).then_inc(ident_ready, 1)

            def root_w(i, tile):
                pool.wait_ge(var_w_ready[i], tile + 1)
                if tile >= 2:
                    pool.wait_ge(xhat_ready[i], tile - 1)
                nc.gpsimd.tensor_tensor(rstd_w[:, i, tile % 2:tile % 2 + 1], var_w[:, i, tile % 2:tile % 2 + 1],
                                        minus_half[:, 0:1],
                                        ALU.pow).then_inc(rstd_w_ready[i], 1)

            def bias(mid):
                if mid is not None:
                    if mid == 0:
                        pool.wait_ge(bout_loaded, 16)
                    pool.wait_ge(xr_loaded[mid % 4], 16 * (mid // 4 + 1))
                    nc.gpsimd.tensor_tensor(xr[:, mid % 4, :], xr[:, mid % 4, :], bout_rows[:, :],
                                            ALU.add).then_inc(xr_biased, 1)

            def root(i, q):
                pool.wait_ge(var_ready[i], q + 1)
                nc.gpsimd.tensor_tensor(rstd[:, i, :], var[:, i, :], minus_half[:, :], ALU.pow).then_inc(rstd_ready[i], 1)

            power_steps = [0]

            def square(lev):
                def step(op, dst, a, b):
                    power_steps[0] += 1
                    op(dst, a, b).then_inc(power_step, 1)

                def settle():
                    pool.wait_ge(power_step, power_steps[0])

                def add(dst, a, b):
                    return nc.gpsimd.tensor_tensor(dst, a, b, ALU.add)

                def sub(dst, a, b):
                    return nc.gpsimd.tensor_tensor(dst, a, b, ALU.subtract)

                def mul(dst, a, b):
                    return nc.gpsimd.tensor_tensor(dst, a, b, ALU.mult)

                sq = [pool_small[:, i, :] for i in range(6)]
                cr, ci = power[:, lev, 0, :], power[:, lev, 1, :]
                step(mul, sq[0], cr, cr)
                step(mul, sq[1], ci, ci)
                step(mul, sq[2], cr, ci)
                settle()
                step(sub, sq[3], sq[0], sq[1])
                step(add, sq[4], sq[0], sq[1])
                step(add, sq[5], sq[2], sq[2])
                settle()
                step(sub, sq[4], two[:, :], sq[4])
                settle()
                step(mul, power[:, lev + 1, 0, :], sq[3], sq[4])
                step(mul, power[:, lev + 1, 1, :], sq[5], sq[4])
                settle()

            table_steps = [0]

            def double_table(lev, l):
                n = 1 << lev
                parts = [bout_rows[:, i * HALF:i * HALF + 2 * n].rearrange("p (c j) -> p c j", c=2) for i in range(2)]
                for i in range(2):
                    nc.gpsimd.tensor_scalar(parts[i], turn[:, l, :, 0:n], power[:, lev, i, l:l + 1], None,
                                            ALU.mult).then_inc(table_step, 1)
                table_steps[0] += 2
                pool.wait_ge(table_step, table_steps[0])
                nc.gpsimd.tensor_tensor(turn[:, l, 0, n:2 * n], parts[0][:, 0, :], parts[1][:, 1, :],
                                        ALU.subtract).then_inc(table_step, 1)
                nc.gpsimd.tensor_tensor(turn[:, l, 1, n:2 * n], parts[0][:, 1, :], parts[1][:, 0, :],
                                        ALU.add).then_inc(table_step, 1)
                table_steps[0] += 2
                pool.wait_ge(table_step, table_steps[0])

            for n in SLOTS:
                m, g, fr = mixer_of(n), final_of(n), fronts_of(n)
                mid, w = middle_of(n), weight_of(n)
                for q in EARLY.get(n, []):
                    root_w(0, q)
                if n == -AHEAD:
                    pool.wait_ge(modulus_squared, 1)
                    nc.gpsimd.tensor_tensor(small[:, 1, :], small[:, 0, :], minus_half[:, 0:LAYERS],
                                            ALU.pow).then_inc(modulus_root, 1)
                    root_w(0, 2)
                    pool.wait_ge(rotation_ready, 1)
                for lev in SQUARES.get(n, []):
                    square(lev)
                if m is not None:
                    root(0, m)
                if n >= 0:
                    for f in fr[2:] if n == 0 else fr[:1]:
                        for q in after(f):
                            root_w(0, q)
                if g is not None:
                    root(2, g)
                if 0 < n <= 2 * (LAYERS - 1):
                    l = (n + 1) // 2
                    if n == 1:
                        pool.wait_ge(tables_shared, 1)
                    for lev in range(SHARED_LEVELS, LEVELS - 1) if n % 2 else range(LEVELS - 1, LEVELS):
                        double_table(lev, l)
                if mid is not None:
                    root_w(1, mid)
                if w is not None:
                    pool.wait_ge(deq_ready, w + 1)
                    pool.wait_ge(w_loaded[w % 2], 32 * (w // 2 + 1))
                    nc.gpsimd.tensor_tensor(w_nat[w % 2], w_deq, w_nat[w % 2], ALU.add).then_inc(w_ready, 1)
                if mlp_of(n + 1) is not None:
                    root(1, mlp_of(n + 1))
                if n > 0:
                    for f in fr[1:]:
                        for q in after(f):
                            root_w(0, q)
                bias(middle_of(n + 1))

        @block.scalar
        def _(act):
            for i, (name, v) in enumerate(vectors[:len(vectors) // 2]):
                act.dma_start(par_rows[PAR[name]:PAR[name] + v.shape[0], :], v).then_inc(params_loaded[i >= FIRST], 16)

            def norm_w(i, tile, dst, src):
                act.wait_ge(shift_w_ready[i], tile + 1)
                nc.scalar.activation(dst, src, ACT.Identity, bias=shift_w[:, i, tile % 2:tile % 2 + 1],
                                     scale=rstd_w[:, i, tile % 2:tile % 2 + 1]).then_inc(xhat_ready[i], 1)

            def normalise(i, q, n):
                b, k = TURN[TOKENS[i], q]
                act.wait_ge(shift_ready[i], shifts(i, q))
                lane = lane_freed(act, i, q, n)
                for r in range(R):
                    last = nc.scalar.activation(normed[:, lane, r, :], bank[b][:, r * P:(r + 1) * P], ACT.Identity,
                                                bias=shift[:, i, r:r + 1], scale=rstd[:, i, r:r + 1])
                last.then_inc(drained[b], 1)

            def front_out(f, u):
                b, k = TURN["front", f, u]
                act.wait_ge(filled[b], k + 1)
                if f % 2 == 0 and f >= 2:
                    bw, kw = TURN["Win", f // 2 - 1]
                    act.wait_ge(filled[bw], kw + 1)
                nc.scalar.activation(xT[:, u * KH:(u + 1) * KH, f % 2 * P:(f % 2 + 1) * P],
                                     bank[b][:, :].rearrange("p (k t) -> p k t", k=KH),
                                     ACT.Copy).then_inc(drained[b], 1)

            prep_to = {"Win": lambda i: WinT[:, i * KH:(i + 1) * KH, :].rearrange("p k d -> p (k d)"),
                       "W1": lambda i: W1_hi[:, i, :], "W2": lambda i: W2T[:, i, :, :].rearrange("p j d -> p (j d)"),
                       "Wout": lambda i: Wout_hi[:, i * HALF:(i + 1) * HALF]}

            def prep_out(i, n):
                what, i = PREP[n][i]
                b, k = TURN["prep", what, i]
                act.wait_ge(filled[b], k + 1)
                nc.scalar.activation(prep_to[what](i), bank[b][:, :], ACT.Copy).then_inc(
                    prep_hi_ready if (what, i) in SPLIT else drained[b], 1)

            def win_out(pair):
                i = pair * 2 // R
                b, k = TURN["Win", pair]
                act.wait_ge(filled[b], k + 1)
                if pair == 0:
                    bp, kp = TURN["params", 1]
                    act.wait_ge(drained[bp], kp + 1)
                if i >= BATCH:
                    act.wait_ge(mixed, STAGES_PER_CHUNK * (i // BATCH - 1) + i % BATCH + 1)
                at = pair * 2 % R * P
                nc.scalar.activation(h_in[:, i % BATCH, at:at + 2 * P], bank[b][:, 0:2 * P], ACT.Identity,
                                     bias=col("bin")).then_inc(drained[b], 1)

            def params_out(i, first, end):
                b, k = TURN["params", i]
                act.wait_ge(filled[b], k + 1)
                nc.scalar.activation(par[:, first:end], bank[b][:, first:end], ACT.Copy).then_inc(drained[b], 1)

            def norm_ahead(f):
                for q in after(f):
                    norm_w(0, q, front_buffer(q), front_buffer(q))
                    if q == 0:
                        params_out(0, 0, PAR_FIRST)

            def front_step(f):
                if f == 0 or f % 2 == 1 and f < TILES_PER_CHUNK - 1:
                    norm_ahead(f)
                front_out(f, 0)
                front_out(f, 1)
                if f == 1:
                    params_out(1, PAR_FIRST, NPAR)
                if f % 2 == 1:
                    if f < TILES_PER_CHUNK - 1:
                        norm_ahead(f + 1)
                    win_out(f // 2)
                if f == TILES_PER_CHUNK - 1:
                    norm_ahead(f)

            def mixer_input(m):
                b, k = TURN["mixer features", m]
                act.wait_ge(filled[b], k + 1)
                if m > 0:
                    act.wait_ge(y_rotated, 2 * m)
                nc.scalar.activation(y[:, :], bank[b][:, :], ACT.Silu, bias=col("ln1_b", layer(m)),
                                     scale=col("ln1_w", layer(m))).then_inc(drained[b], 1)

            for n in SLOTS:
                m, c, g = mixer_of(n), mlp_of(n), final_of(n)
                fr, mid, w = fronts_of(n), middle_of(n), weight_of(n)
                if n <= 0:
                    front_step(fr[0])
                if n == -3:
                    act.wait_ge(modulus_ready, 1)
                    nc.scalar.activation(decay[:, :], small[:, 2, :], ACT.Tanh).then_inc(decay_ready, 1)
                if c is not None:
                    normalise(1, c, n)
                    b, k = TURN["mlp features", c]
                    act.wait_ge(filled[b], k + 1)
                    if c > 0:
                        bw, kw = TURN["W1", c - 1, FT - 1]
                        act.wait_ge(filled[bw], kw + 1)
                    nc.scalar.activation(yn_hi[:, :], bank[b][:, :], ACT.Identity, bias=col("ln2_b", layer(c)),
                                         scale=col("ln2_w", layer(c))).then_inc(yn_hi_ready, 1)
                    if c > 0:
                        act.wait_ge(yn_lo_ready, c)
                        if final_of(n - 1) is not None:
                            act.wait_ge(fin_lo_ready, final_of(n - 1) + 1)
                    nc.scalar.activation(yn[:, :], bank[b][:, :], ACT.Identity, bias=col("ln2_b", layer(c)),
                                         scale=col("ln2_w", layer(c))).then_inc(drained[b], 1)
                if filling(n) and win_of(n) is not None:
                    win_out(win_of(n))
                if m is not None and not filling(n):
                    normalise(0, m, n)
                if m is not None:
                    mixer_input(m)
                if g is not None and not filling(n):
                    normalise(2, g, n)
                if n <= 0:
                    for f in fr[1:]:
                        front_step(f)
                if not filling(n) and win_of(n) is not None:
                    win_out(win_of(n))
                if c is not None:
                    for j in range(FT):
                        b, k = TURN["W1", c, j]
                        act.wait_ge(filled[b], k + 1)
                        if j >= 2:
                            act.wait_ge(ff_used, (FT - 1) * c + j - 1)
                        elif c > 0:
                            bw, kw = TURN["W2", c - 1]
                            act.wait_ge(filled[bw], kw + 1)
                        nc.scalar.activation(ff[:, j % 2, :], bank[b][:, :], ACT.Silu,
                                             bias=col("b1", layer(c) * FT + j)).then_inc(drained[b], 1)
                        if j in (1, 2) and fr:
                            front_out(fr[0], j - 1)
                        if j == 1 and w is not None:
                            act.wait_ge(offsets_ready, w + 1)
                            nc.scalar.activation(w_deq, offsets.rearrange("p i two -> p (i two)"), ACT.Identity,
                                                 bias=minus_8_scales[:, w:w + 1],
                                                 scale=col("scales", w)).then_inc(deq_ready, 1)
                if g is not None and filling(n):
                    normalise(2, g, n)
                if mid is not None:
                    if m is not None:
                        act.wait_ge(mixed, m + 1)
                    if mid > 0:
                        bw, kw = TURN["middle", mid - 1, 1]
                        act.wait_ge(filled[bw], kw + 1)
                    norm_w(1, mid, xhat, xr[:, mid % 4, :])
                if n > 0:
                    for f in fr[:1]:
                        norm_ahead(f)
                    for f in fr[1:]:
                        front_out(f, 0)
                        front_out(f, 1)
                        norm_ahead(f)
                if mid is not None:
                    for u in range(2):
                        b, k = TURN["middle", mid, u]
                        act.wait_ge(filled[b], k + 1)
                        if mid >= 2 and u == 0:
                            bw, kw = TURN["back", mid - 2, 1]
                            act.wait_ge(filled[bw], kw + 1)
                        nc.scalar.activation(x_hi[:, mid % 2, u * KH:(u + 1) * KH, :].rearrange("p k t -> p (k t)"),
                                             bank[b][:, :], ACT.Copy).then_inc(x_hi_ready, 1)
                if w is not None:
                    for u in range(2):
                        b, k = TURN["weight", w, u]
                        act.wait_ge(filled[b], k + 1)
                        nc.scalar.activation(w_hi[:, u * KH:(u + 1) * KH, w * P:(w + 1) * P],
                                             bank[b][:, :].rearrange("p (k o) -> p k o", k=KH),
                                             ACT.Copy).then_inc(w_hi_ready, 1)
                if g is not None:
                    b, k = TURN["final features", g]
                    act.wait_ge(filled[b], k + 1)
                    if c is not None:
                        act.wait_ge(yn_lo_ready, c + 1)
                    elif final_of(n - 1) is not None:
                        act.wait_ge(fin_lo_ready, g)
                    nc.scalar.activation(yn[:, :], bank[b][:, :], ACT.Identity, bias=col("lnl_b"),
                                         scale=col("lnl_w")).then_inc(fin_hi_ready, 1)
                    if g >= BATCH:
                        last = TILES_PER_CHUNK * (g // BATCH - 1) + R * (g % BATCH) + R - 1
                        bw, kw = TURN["Wout", last, 1]
                        act.wait_ge(filled[bw], kw + 1)
                    nc.scalar.activation(fin_hi[:, g % BATCH, :], bank[b][:, :], ACT.Identity, bias=col("lnl_b"),
                                         scale=col("lnl_w")).then_inc(drained[b], 1)
                for i in range(len(PREP.get(n, []))):
                    prep_out(i, n)

        @block.vector
        def _(dve):
            steps = [0]

            def step(ins):
                steps[0] += 1
                ins.then_inc(vec_step, 1)
                return steps[0]

            def settle(count=None):
                dve.wait_ge(vec_step, steps[0] if count is None else count)

            vv = nc.vector

            def s(i):
                return small[:, i, :]

            def find_rotation():
                b, k = TURN["params", 0]
                dve.wait_ge(drained[b], k + 1)
                re, im = (par[:, PAR[q]:PAR[q] + LAYERS] for q in ("phz_re", "phz_im"))
                step(vv.tensor_tensor(s(3), re, re, ALU.mult))
                step(vv.tensor_tensor(s(4), im, im, ALU.mult))
                settle()
                step(vv.tensor_tensor(s(5), s(3), s(4), ALU.add))
                settle()
                vv.tensor_scalar(s(0), s(5), 1e-36, None, ALU.max).then_inc(modulus_squared, 1)
                step(vv.tensor_scalar(s(6), s(5), 1e-36, None, ALU.is_lt))
                dve.wait_ge(modulus_root, 1)
                settle()
                vv.tensor_tensor(s(2), s(5), s(1), ALU.mult).then_inc(modulus_ready, 1)
                step(vv.tensor_tensor(s(7), re, s(1), ALU.mult))
                step(vv.tensor_tensor(s(8), im, s(1), ALU.mult))
                step(vv.tensor_scalar(s(9), s(6), -1.0, 1.0, ALU.mult, ALU.add))
                settle()
                step(vv.tensor_tensor(s(7), s(7), s(9), ALU.mult))
                step(vv.tensor_tensor(s(8), s(8), s(9), ALU.mult))
                settle()
                step(vv.tensor_tensor(power[:, 0, 0, :], s(7), s(6), ALU.add))
                step(vv.tensor_scalar(power[:, 0, 1, :], s(8), -1.0, None, ALU.mult))
                settle()
                step(vv.tensor_tensor(s(10), power[:, 0, 0, :], power[:, 0, 0, :], ALU.mult))
                step(vv.tensor_tensor(s(11), power[:, 0, 1, :], power[:, 0, 1, :], ALU.mult))
                settle()
                step(vv.tensor_tensor(s(12), s(10), s(11), ALU.add))
                settle()
                step(vv.tensor_scalar(s(12), s(12), -0.5, 1.5, ALU.mult, ALU.add))
                settle()
                step(vv.tensor_tensor(power[:, 0, 0, :], power[:, 0, 0, :], s(12), ALU.mult))
                step(vv.tensor_tensor(power[:, 0, 1, :], power[:, 0, 1, :], s(12), ALU.mult))
                settle()
                lr, li = (par[:, PAR[q]:PAR[q] + LAYERS] for q in ("lc_re", "lc_im"))
                er, ei = power[:, 0, 0, :], power[:, 0, 1, :]
                step(vv.tensor_tensor(s(10), er, lr, ALU.mult))
                step(vv.tensor_tensor(s(11), ei, li, ALU.mult))
                step(vv.tensor_tensor(s(12), er, li, ALU.mult))
                step(vv.tensor_tensor(s(13), ei, lr, ALU.mult))
                settle()
                for st in range(BATCH):
                    step(vv.tensor_tensor(state[:, :, st, 0], s(10), s(11), ALU.add))
                    step(vv.tensor_tensor(state[:, :, st, 1], s(12), s(13), ALU.subtract))
                step(vv.memset(turn[:, :, 0, 0:1], 1.0))
                step(vv.memset(turn[:, :, 1, 0:1], 0.0))
                settle()
                vv.memset(small[:, 13, :], 0.0).then_inc(rotation_ready, 1)

            def double_table(lev, l0, l1):
                n, nl = 1 << lev, l1 - l0
                src = turn[:, l0:l1, :, 0:n]
                parts = [double_early[:, i * HALF:i * HALF + nl * 2 * n].rearrange("p (l c j) -> p l c j", l=nl, c=2) for i in range(2)]
                for i in range(2):
                    by = power[:, lev, i, l0:l1].rearrange("p (l c j) -> p l c j", c=1, j=1)
                    step(vv.tensor_tensor(parts[i], src, by.to_broadcast([P, nl, 2, n]), ALU.mult))
                settle()
                step(vv.tensor_tensor(turn[:, l0:l1, 0, n:2 * n], parts[0][:, :, 0, :], parts[1][:, :, 1, :],
                                      ALU.subtract))
                step(vv.tensor_tensor(turn[:, l0:l1, 1, n:2 * n], parts[0][:, :, 1, :], parts[1][:, :, 0, :],
                                      ALU.add))
                settle()

            def stats_w(i, tile, src):
                for u in range(2):
                    step(vv.bn_stats(bn_w[:, i, u, :], src[:, u * HALF:(u + 1) * HALF]))
                settle()
                step(vv.bn_aggr(mv_w[:, i, tile % 2, :], bn_w[:, i, :, :].rearrange("p a b -> p (a b)")))
                settle()
                vv.tensor_scalar(var_w[:, i, tile % 2:tile % 2 + 1], mv_w[:, i, tile % 2, 1:2], EPS, None, ALU.add).then_inc(var_w_ready[i], 1)

            def find_shift_w(i, tile):
                dve.wait_ge(rstd_w_ready[i], tile + 1)
                vv.scalar_tensor_tensor(shift_w[:, i, tile % 2:tile % 2 + 1], mv_w[:, i, tile % 2, 0:1], -1.0,
                                        rstd_w[:, i, tile % 2:tile % 2 + 1], ALU.mult, ALU.mult).then_inc(shift_w_ready[i], 1)

            def stats(i, q):
                b, k = TURN[TOKENS[i], q]
                dve.wait_ge(filled[b], k + 1)
                for r in range(R):
                    step(vv.bn_stats(bn[:, i, r, :], bank[b][:, r * P:(r + 1) * P]))
                settle()
                for r in range(R):
                    step(vv.bn_aggr(mv[:, i, r, :], bn[:, i, r, :]))
                settle()
                vv.tensor_scalar(var[:, i, :], mv[:, i, :, 1], EPS, None, ALU.add).then_inc(var_ready[i], 1)

            def find_shift(i, q):
                dve.wait_ge(rstd_ready[i], q + 1)
                vv.scalar_tensor_tensor(shift[:, i, :], mv[:, i, :, 0], -1.0, rstd[:, i, :], ALU.mult,
                                        ALU.mult).then_inc(shift_ready[i], 1)

            def normalise(i, q, n):
                b, k = TURN[TOKENS[i], q]
                lane = lane_freed(dve, i, q, n)
                dve.wait_ge(rstd_ready[i], q + 1)
                for r in range(R):
                    last = vv.tensor_scalar(normed[:, lane, r, :], bank[b][:, r * P:(r + 1) * P], mv[:, i, r, 0:1],
                                            rstd[:, i, r:r + 1], ALU.subtract, ALU.mult)
                last.then_inc(drained[b], 1)

            def residual(key, u, t):
                b, k = TURN[key, t, u]
                dve.wait_ge(filled[b], k + 1)
                at = xr[:, t % 4, u * HALF:(u + 1) * HALF]
                vv.tensor_tensor(at, bank[b][:, :], at, ALU.add).then_inc(drained[b], 1)

            def front_stats(f, shift=True):
                tiles_stats(after(f), shift)

            def tiles_stats(tiles, shift=True):
                for q in tiles:
                    if q < TILES_PER_CHUNK:
                        dve.wait_ge(x_first_loaded[q], 16)
                    else:
                        dve.wait_ge(x_loaded[q % 2], 16 * ((q - TILES_PER_CHUNK) // 2 + 1))
                    stats_w(0, q, front_buffer(q))
                for q in tiles if shift else []:
                    find_shift_w(0, q)

            def front_shift(f):
                for q in after(f):
                    find_shift_w(0, q)

            def prep_lo(n):
                for what, i in PREP.get(n, []):
                    if (what, i) in SPLIT:
                        b, k = TURN["prep", what, i]
                        dve.wait_ge(prep_hi_ready, SPLIT.index((what, i)) + 1)
                        cols = slice(i * HALF, (i + 1) * HALF)
                        hi, lo = ((W1_hi[:, i, :], W1_lo[:, i, :]) if what == "W1" else
                                  (Wout_hi[:, cols], Wout_lo[:, cols]))
                        vv.tensor_tensor(lo, bank[b][:, :], hi.bitcast(fp32), ALU.subtract).then_inc(drained[b], 1)

            def add_mlp(c):
                b, k = TURN["W2", c]
                dve.wait_ge(filled[b], k + 1)
                dve.wait_ge(mixed, c + 1)
                vv.scalar_tensor_tensor(h[:, stream(c), :], bank[b][:, :], col("b2", layer(c)),
                                        h[:, stream(c), :], ALU.add, ALU.add).then_inc(drained[b], 1)

            def weight_lo(before):
                for u in range(2):
                    b, k = TURN["weight", before, u]
                    dve.wait_ge(w_hi_ready, 2 * before + u + 1)
                    at, cols = slice(u * KH, (u + 1) * KH), slice(before * P, (before + 1) * P)
                    vv.tensor_tensor(w_lo[:, at, cols], bank[b][:, :].rearrange("p (k o) -> p k o", k=KH),
                                     w_hi[:, at, cols].bitcast(fp32), ALU.subtract).then_inc(drained[b], 1)

            for n in SLOTS:
                m, c, g, fr = mixer_of(n), mlp_of(n), final_of(n), fronts_of(n)
                mid, bk, w = middle_of(n), back_of(n), weight_of(n)
                tiles_stats(EARLY.get(n, []))
                if n == -1:
                    prep_lo(-2)
                if c is not None and not filling(n):
                    find_shift(1, c)
                before = middle_of(n - 1)
                if before is not None:
                    for u in range(2):
                        b, k = TURN["middle", before, u]
                        dve.wait_ge(x_hi_ready, 2 * before + u + 1)
                        at = slice(u * KH, (u + 1) * KH)
                        vv.tensor_tensor(x_lo[:, before % 2, at, :].rearrange("p k t -> p (k t)"), bank[b][:, :],
                                         x_hi[:, before % 2, at, :].rearrange("p k t -> p (k t)").bitcast(fp32),
                                         ALU.subtract).then_inc(drained[b], 1)
                if m is not None:
                    stats(0, m)
                if filling(n):
                    find_shift(1, c)
                before = back_of(n - 1)
                if before is not None:
                    residual("back", 1, before)
                if filling(n):
                    for f in fr[:1]:
                        front_stats(f, False)
                before = final_of(n - 1)
                if before is not None:
                    b, k = TURN["final features", before]
                    dve.wait_ge(drained[b], k + 1)
                    dve.wait_ge(fin_hi_ready, before + 1)
                    vv.tensor_tensor(fin_lo[:, before % BATCH, :], yn[:, :],
                                     fin_hi[:, before % BATCH, :].bitcast(fp32), ALU.subtract).then_inc(fin_lo_ready, 1)
                before = weight_of(n - 1)
                if before is not None and mid is not None:
                    weight_lo(before)
                if m is not None:
                    normalise(0, m, n) if filling(n) else find_shift(0, m)
                if g is not None:
                    stats(2, g)
                if n == 0:
                    front_stats(fr[2])
                elif n > 0 and not filling(n):
                    for f in fr[:1]:
                        front_stats(f)
                if g is not None and not filling(n):
                    find_shift(2, g)
                if filling(n):
                    for f in fr[:1]:
                        front_shift(f)
                if c is not None:
                    dve.wait_ge(yn_hi_ready, c + 1)
                    b, k = TURN["mlp features", c]
                    dve.wait_ge(drained[b], k + 1)
                    if c > 0:
                        b, k = TURN["W1", c - 1, FT - 1]
                        dve.wait_ge(filled[b], k + 1)
                    vv.tensor_tensor(yn_lo[:, :], yn[:, :], yn_hi[:, :].bitcast(fp32),
                                     ALU.subtract).then_inc(yn_lo_ready, 1)
                if n == 1:
                    prep_lo(0)
                before = weight_of(n - 1)
                if before is not None and mid is None:
                    weight_lo(before)
                if mid is not None:
                    dve.wait_ge(xr_biased, mid + 1)
                    residual("Wout", 0, mid)
                    residual("Wout", 1, mid)
                    b, k = TURN["Wout", mid, 1]
                    dve.wait_ge(drained[b], k + 1)
                    stats_w(1, mid, xr[:, mid % 4, :])
                if n == -AHEAD:
                    find_rotation()
                    tiles_stats([2])
                for lev in DOUBLINGS.get(n, []):
                    if lev > 0:
                        dve.wait_ge(power_step, POWER_STEPS * lev)
                    double_table(lev, 0, LAYERS if lev < SHARED_LEVELS else 1)
                if n == 0:
                    b, k = TURN["params", 1]
                    dve.wait_ge(drained[b], k + 1)
                    vv.tensor_scalar(minus_8_scales[:, :], par[:, PAR["scales"]:PAR["scales"] + OT], -8.0, None,
                                     ALU.mult).then_inc(tables_shared, 1)
                if w is not None:
                    dve.wait_ge(w_loaded[w % 2], 32 * (w // 2 + 1))
                    nib = nibbles_in[w % 2]
                    if w > 0:
                        dve.wait_ge(w_ready, w)
                    vv.tensor_scalar(offsets[:, :, 0], nib, 15, None, ALU.bitwise_and)
                    vv.tensor_scalar(offsets[:, :, 1], nib, 4, 15, ALU.logical_shift_right,
                                     ALU.bitwise_and).then_inc(offsets_ready, 1)
                if m is not None:
                    l, st = layer(m), stream(m)
                    b, k = TURN["mixer features", m]
                    dve.wait_ge(drained[b], k + 1)
                    if m == 0:
                        dve.wait_ge(decay_ready, 1)
                    if 0 < l and m < STAGES_PER_CHUNK and st == 0:
                        dve.wait_ge(table_step, TABLE_STEPS * (LEVELS - SHARED_LEVELS) * l)
                    if mid is not None and mid > 0:
                        b, k = TURN["middle", mid - 1, 1]
                        dve.wait_ge(filled[b], k + 1)
                    for part in range(2):
                        vv.tensor_tensor(z[:, part, :], y[:, :], turn[:, l, part, :], ALU.mult).then_inc(y_rotated, 1)
                if g is not None and filling(n):
                    find_shift(2, g)
                if m is not None:
                    scans = []
                    for part in range(2):
                        dve.wait_ge(y_rotated, 2 * m + part + 1)
                        scans.append(step(vv.tensor_tensor_scan(
                            z[:, part, :], decay[:, l:l + 1].to_broadcast([P, CHUNK]), z[:, part, :],
                            state[:, l, st, part:part + 1], ALU.mult, ALU.add)))
                if m is not None:
                    settle(scans[1])
                    cr, ci = power[:, LEVELS, 0, l:l + 1], power[:, LEVELS, 1, l:l + 1]
                    z0, z1 = z[:, 0, CHUNK - 1:CHUNK], z[:, 1, CHUNK - 1:CHUNK]
                    step(vv.tensor_tensor(s(10)[:, 0:1], z1, ci, ALU.mult))
                    step(vv.tensor_tensor(s(11)[:, 0:1], z0, ci, ALU.mult))
                    step(vv.tensor_tensor(s(12)[:, 0:1], z0, cr, ALU.mult))
                    first = step(vv.tensor_tensor(s(13)[:, 0:1], z1, cr, ALU.mult))
                    settle(first)
                    back = [step(vv.tensor_tensor(z[:, part, :], z[:, part, :], turn[:, l, part, :], ALU.mult))
                            for part in range(2)]
                    step(vv.tensor_tensor(state[:, l, st, 0:1], s(12)[:, 0:1], s(10)[:, 0:1], ALU.add))
                    step(vv.tensor_tensor(state[:, l, st, 1:2], s(13)[:, 0:1], s(11)[:, 0:1], ALU.subtract))
                    src = h_in if l == 0 else h
                    if l > 0:
                        b, k = TURN["W2", m - BATCH]
                        dve.wait_ge(drained[b], k + 1)
                    settle(back[0])
                    step(vv.scalar_tensor_tensor(h[:, st, :], z[:, 0, :], col("scl", l), src[:, st, :],
                                                 ALU.mult, ALU.add))
                    settle()
                    vv.scalar_tensor_tensor(h[:, st, :], z[:, 1, :], col("scl", l), h[:, st, :],
                                            ALU.mult, ALU.add).then_inc(mixed, 1)
                if mid is not None:
                    find_shift_w(1, mid)
                if bk is not None:
                    residual("back", 0, bk)
                if n == 0:
                    prep_lo(-1)
                if filling(n):
                    add_mlp(c)
                if mlp_of(n + 1) is not None:
                    stats(1, mlp_of(n + 1))
                if c is not None and not filling(n):
                    add_mlp(c)
                if n >= 0:
                    for f in fr[3:] if n == 0 else fr[1:]:
                        front_stats(f)

        @block.tensor
        def _(pe):
            mm, tr = nc.tensor.matmul, nc.tensor.transpose

            def claim(*key):
                b, k = TURN[key]
                if k > 0:
                    pe.wait_ge(drained[b], k)
                return bank[b], filled[b]

            def drained_of(*key):
                b, k = TURN[key]
                pe.wait_ge(drained[b], k + 1)

            pe.wait_ge(ident_ready, 1)

            def to_tokens(key, src):
                ps, full = claim(*key)
                for r in range(R):
                    last = tr(ps[:, r * P:(r + 1) * P], src[:, r * P:(r + 1) * P], ident[:, :])
                last.then_inc(full, 1)

            def to_features(key, lane, token_key):
                ps, full = claim(*key)
                drained_of(*token_key)
                for r in range(R):
                    last = tr(ps[:, r * P:(r + 1) * P], normed[:, lane, r, :], ident[:, :])
                last.then_inc(full, 1)

            def width_transpose(key, src, u):
                ps, full = claim(*key)
                for i in range(KH):
                    q = u * KH + i
                    last = tr(ps[:, i * P:(i + 1) * P], src[:, q * P:(q + 1) * P], ident[:, :])
                last.then_inc(full, 1)

            def three_pass(ps, hi, lo, w_h, w_l, first, last):
                mm(ps, hi, w_h, start=first, stop=False)
                mm(ps, hi, w_l, start=False, stop=False)
                return mm(ps, lo, w_h, start=False, stop=last)

            def big(bk, u, q0, q1):
                b, k = TURN["back", bk, u]
                cols = slice(u * HALF, (u + 1) * HALF)
                if q0 == 0:
                    claim("back", bk, u)
                for q in range(q0, q1):
                    last = three_pass(bank[b][:, :], x_hi[:, bk % 2, q, :], x_lo[:, bk % 2, q, :],
                                      w_hi[:, q, cols], w_lo[:, q, cols], q == 0, q == K - 1)
                if q1 == K:
                    last.then_inc(filled[b], 1)

            def wout(mid, u):
                ps, full = claim("Wout", mid, u)
                st, r = mid % TILES_PER_CHUNK // R, mid % R
                at, cols = slice(r * P, (r + 1) * P), slice(u * HALF, (u + 1) * HALF)
                pe.wait_ge(fin_lo_ready, BATCH * (mid // TILES_PER_CHUNK) + st + 1)
                three_pass(ps[:, :], fin_hi[:, st, at], fin_lo[:, st, at], Wout_hi[:, cols], Wout_lo[:, cols],
                           True, True).then_inc(full, 1)

            nat = {"Win": lambda i, q: Win_nat[:, (i * KH + q) * P:(i * KH + q + 1) * P],
                   "W1": lambda i, q: W1_nat[:, i, q, :], "W2": lambda i, q: W2_nat[:, i, q * P:(q + 1) * P],
                   "Wout": lambda i, q: Wout_nat[:, i * KH + q, :]}

            def params(i, n):
                ps, full = claim("params", i)
                tr(ps[:, 0:n], par_rows[0:n, :], ident[0:n, 0:n]).then_inc(full, 1)

            def front_in(f):
                pe.wait_ge(xhat_ready[0], f + 1)
                width_transpose(("front", f, 0), front_buffer(f), 0)
                width_transpose(("front", f, 1), front_buffer(f), 1)

            def win(pair, q0=0, q1=K):
                b, k = TURN["Win", pair]
                if q0 == 0:
                    drained_of("prep", "Win", 0)
                    drained_of("prep", "Win", 1)
                    drained_of("front", 2 * pair + 1, 0)
                    drained_of("front", 2 * pair + 1, 1)
                    claim("Win", pair)
                for q in range(q0, q1):
                    last = mm(bank[b][:, 0:2 * P], WinT[:, q, :], xT[:, q, :], start=(q == 0), stop=(q == K - 1))
                if q1 == K:
                    last.then_inc(filled[b], 1)

            def prep(n):
                for what, i in PREP.get(n, []):
                    pe.wait_ge(nat_loaded[what], 16)
                    ps, full = claim("prep", what, i)
                    for q in range(KH):
                        last = tr(ps[:, q * P:(q + 1) * P], nat[what](i, q), ident[:, :])
                    last.then_inc(full, 1)

            def mlp_tokens(c):
                pe.wait_ge(mixed, c + 1)
                to_tokens(("mlp tokens", c), h[:, stream(c), :])

            def front_step(f):
                front_in(f)
                if f == TILES_PER_CHUNK - 1:
                    mlp_tokens(0)
                if f == 1:
                    pe.wait_ge(params_loaded[1], 16 * (len(vectors) - FIRST))
                    params(1, NPAR)
                if f % 2 == 1:
                    win(f // 2)

            pe.wait_ge(params_loaded[0], 16 * FIRST)
            params(0, PAR_FIRST)
            for n in SLOTS:
                m, c, g, fr = mixer_of(n), mlp_of(n), final_of(n), fronts_of(n)
                mid, bk, w = middle_of(n), back_of(n), weight_of(n)
                if n <= 0:
                    front_step(fr[0])
                if bk is not None:
                    drained_of("middle", bk, 0)
                    drained_of("middle", bk, 1)
                    if bk == 0:
                        drained_of("weight", OT - 1, 0)
                        drained_of("weight", OT - 1, 1)
                if bk == 0:
                    big(bk, 0, 0, KH)
                if c is not None:
                    to_features(("mlp features", c), 1, ("mlp tokens", c))
                if g is not None:
                    drained_of("W2", n - BATCH)
                    to_tokens(("final tokens", g), h[:, g % BATCH, :])
                if filling(n) and win_of(n) is not None:
                    win(win_of(n), KH, K)
                if bk is not None and bk > 0:
                    big(bk, 0, 0, KH)
                if mid is not None:
                    wout(mid, 0)
                    wout(mid, 1)
                if m is not None and not filling(n):
                    to_features(("mixer features", m), 0, ("mixer tokens", m))
                if bk is not None:
                    big(bk, 0, KH, K)
                if not filling(n) and win_of(n) is not None:
                    win(win_of(n))
                if bk is not None:
                    big(bk, 1, 0, KH)
                if n <= 0:
                    for f in fr[1:]:
                        front_step(f)

                if c is not None:
                    pe.wait_ge(yn_hi_ready, c + 1)

                    def mlp_in(*pieces):
                        for j in pieces:
                            ps, full = claim("W1", c, j)
                            at = slice(j * P, (j + 1) * P)
                            mm(ps[:, :], W1_hi[:, layer(c), at], yn_hi[:, :], start=True, stop=False)
                            mm(ps[:, :], W1_lo[:, layer(c), at], yn_hi[:, :], start=False, stop=False)
                        if 0 in pieces:
                            if m is not None and filling(n):
                                to_features(("mixer features", m), 0, ("mixer tokens", m))
                            pe.wait_ge(yn_lo_ready, c + 1)
                        for j in pieces:
                            b, k = TURN["W1", c, j]
                            mm(bank[b][:, :], W1_hi[:, layer(c), j * P:(j + 1) * P], yn_lo[:, :], start=False,
                               stop=True).then_inc(filled[b], 1)

                    mlp_in(0, 1)
                    for f in fr[:1]:
                        front_in(f)
                    b, k = TURN["W2", c]
                    claim("W2", c)
                    for j in range(FT):
                        drained_of("W1", c, j)
                        mm(bank[b][:, :], W2T[:, layer(c), j, :], ff[:, j % 2, :], start=(j == 0),
                           stop=(j == FT - 1)).then_inc(ff_used if j < FT - 1 else filled[b], 1)
                        if j + 2 < FT:
                            mlp_in(j + 2)
                        if j == (FT - 1 if filling(n) else 1):
                            if mlp_of(n + 1) is not None:
                                mlp_tokens(mlp_of(n + 1))
                    for f in fr[1:]:
                        front_in(f)
                if mid is not None:
                    pe.wait_ge(xhat_ready[1], mid + 1)
                    for u in range(2):
                        width_transpose(("middle", mid, u), xhat, u)
                next_m = mixer_of(n + 1)
                if next_m is not None:
                    if layer(next_m) == 0:
                        drained_of("Win", 2 * (BATCH * (next_m // STAGES_PER_CHUNK) + stream(next_m)) + 1)
                        to_tokens(("mixer tokens", next_m), h_in[:, stream(next_m), :])
                    else:
                        drained_of("W2", next_m - BATCH)
                        to_tokens(("mixer tokens", next_m), h[:, stream(next_m), :])
                if w is not None:
                    pe.wait_ge(w_ready, w + 1)
                    for u in range(2):
                        width_transpose(("weight", w, u), w_nat[w % 2], u)
                if g is not None:
                    to_features(("final features", g), 1, ("final tokens", g))
                if filling(n) and filling(n + 1) and win_of(n + 1) is not None:
                    win(win_of(n + 1), 0, KH)
                prep(n)
                if bk is not None:
                    big(bk, 1, KH, K)


def kernel(**inputs):
    import numpy as _np
    import concourse.bacc as _bacc
    from concourse import mybir as _mybir
    from concourse.bass_utils import run_bass_kernel_spmd as _run

    nc = _bacc.Bacc("TRN2", target_bir_lowering=False, num_devices=1)
    arrays, args = {}, []
    for name in _INS:
        a = _np.ascontiguousarray(inputs[name])
        arrays[f"in_{name}_dram"] = a
        args.append(nc.dram_tensor(f"in_{name}_dram", a.shape, _mybir.dt.from_np(a.dtype), kind="ExternalInput").ap())
    for i, (shape, dtype) in enumerate(_OUTS):
        dt = _mybir.dt.from_np(_np.dtype(dtype))
        args.append(nc.dram_tensor(f"out_{i}_dram", shape, dt, kind="ExternalOutput").ap())
    sequence_block(nc, *args)
    r = _run(nc, [arrays], core_ids=[0])
    got = tuple(r.results[0][f"out_{i}_dram"] for i in range(len(_OUTS)))
    return got[0]
```
